# Optimizing a Trainium2 kernel written in Bass

```python
import numpy as np
import jax
import jax.numpy as jnp

def _softmax(x, axis=-1):
    return jax.nn.softmax(x, axis=axis)

def _gelu(x):
    return jax.nn.gelu(x, approximate=True)

def _silu(x):
    return jax.nn.silu(x)

def _sigmoid(x):
    return jax.nn.sigmoid(x)

def _layernorm(x, axis=-1, eps=1e-05):
    m = jnp.mean(x, axis=axis, keepdims=True)
    v = jnp.var(x, axis=axis, keepdims=True)
    return (x - m) / jnp.sqrt(v + eps)

def _scatter_add(tgt, idx, src, axis=0):
    return tgt.at[idx].add(src)

def _segment_sum(src, seg, n):
    return jax.ops.segment_sum(src, seg, n)
kernel_name = 'mk_flamingo_gated_d1_seqx_r8_882a5d'

def setup_inputs(seed: int=0):
    np.random.seed(seed)
    _w = jnp.asarray

    def _rec_inputs():
        import jax
        import jax.numpy as jnp
        _rk = jax.random.key(seed)
        x = 7.22e-05 + 1 * jax.random.normal(jax.random.fold_in(_rk, 1), (32, 128, 128), jnp.float32)
        _lenS = 128 - jax.random.randint(jax.random.fold_in(_rk, 7), (32,), 0, max(1, 128 // 4) + 1, jnp.int32)
        _lenS2 = 77 - jax.random.randint(jax.random.fold_in(_rk, 8), (32,), 0, max(1, 77 // 4) + 1, jnp.int32)
        _ctx_768P = jax.random.normal(jax.random.fold_in(_rk, 11), (32, 16, 96), jnp.float32)
        _ctx_768c = jax.random.dirichlet(jax.random.fold_in(_rk, 511), 0.3 * jnp.ones((16,), jnp.float32), (32, 77))
        _ctx_768t = jnp.einsum('bsk,bkd->bsd', _ctx_768c, _ctx_768P)
        _ctx_768t = _ctx_768t * jax.lax.rsqrt(jnp.mean(jnp.square(_ctx_768t)) + 1e-12) * 0.953939
        ctx_768 = 3.88148e-05 + 0.999967 * (_ctx_768t + 0.3 * jax.random.normal(jax.random.fold_in(_rk, 611), (32, 77, 96), jnp.float32))
        _validS = jnp.arange(128)[None, :] < _lenS[:, None]
        _validS2 = jnp.arange(77)[None, :] < _lenS2[:, None]
        _causal = jnp.tril(jnp.ones((128, 128), dtype=bool))
        mask_BxS_bf1 = jnp.ones((32, 128), dtype=bool)
        mask_BxS2_bf1 = jnp.ones((32, 77), dtype=bool)
        _g = jax.random.normal(jax.random.fold_in(_rk, 9001), (2, 1), jnp.float32)
        _g = jnp.sign(_g) * jnp.maximum(jnp.abs(_g), 1.0) + (_g == 0) * 1.0
        g_xattn = _g[0]
        g_ffn = _g[1]
        return (x, ctx_768, mask_BxS_bf1, mask_BxS2_bf1, g_xattn, g_ffn)
    x, ctx_768, mask_BxS_bf1, mask_BxS2_bf1, g_xattn, g_ffn = _rec_inputs()

    def _L0_xattn_setup():
        import jax, jax.numpy as jnp
        import numpy as np
        B, T, DT, G, DV = (16, 64, 128, 72, 96)
        H, DH = (4, 32)
        INNER = H * DH
        HID = 4 * DT
        N_STATE = 64
        K_TOP = 32

        def layernorm(x, g, b, eps=1e-05):
            m = x.mean(-1, keepdims=True)
            v = x.var(-1, keepdims=True)
            return (x - m) * jax.lax.rsqrt(v + eps) * g + b

        def s4d(x, log_dt, A_re, A_im, C_re, C_im, D_skip):
            Bb, L, D = x.shape
            dt = jnp.exp(log_dt)
            A = A_re + 1j * A_im
            C = C_re + 1j * C_im
            dtA = dt[:, None] * A
            dC = C * (jnp.exp(dtA) - 1.0) / A
            powers = jnp.exp(dtA[:, :, None] * jnp.arange(L))
            K = 2.0 * jnp.einsum('dn,dnl->dl', dC, powers).real
            n = 2 * L
            Kf = jnp.fft.rfft(K, n=n, axis=-1)
            xf = jnp.fft.rfft(x, n=n, axis=1)
            y = jnp.fft.irfft(xf * Kf.T[None], n=n, axis=1)[:, :L]
            return y + x * D_skip
        key = jax.random.key(seed)
        ks = jax.random.split(key, 16)
        s = 0.02
        inp = {'x_text': jax.random.normal(ks[0], (B, T, DT), jnp.float32), 'x_vision': jax.random.normal(ks[1], (B, G, DV), jnp.float32), 'text_mask': jnp.ones((B, T), bool), 'vision_mask': jnp.ones((B, G), bool), 'Wq': jax.random.normal(ks[2], (DT, INNER), jnp.float32) * s, 'Wk': jax.random.normal(ks[3], (DV, INNER), jnp.float32) * s, 'Wv': jax.random.normal(ks[4], (DV, DT), jnp.float32) * s, 'W_film_in': jax.random.normal(ks[5], (DT, 2 * DT), jnp.float32) * s, 'b_film_in': jnp.zeros((2 * DT,), jnp.float32), 'W_film_out': jax.random.normal(ks[6], (DT, 2 * DT), jnp.float32) * s, 'b_film_out': jnp.zeros((2 * DT,), jnp.float32), 'g_norm_in': jnp.ones((DT,), jnp.float32), 'b_norm_in': jnp.zeros((DT,), jnp.float32), 'g_norm_out': jnp.ones((DT,), jnp.float32), 'b_norm_out': jnp.zeros((DT,), jnp.float32), 'g_ffn': jnp.ones((DT,), jnp.float32), 'b_ffn': jnp.zeros((DT,), jnp.float32), 'W1': jax.random.normal(ks[7], (DT, HID), jnp.float32) * s, 'b1': jnp.zeros((HID,), jnp.float32), 'W2': jax.random.normal(ks[8], (HID, DT), jnp.float32) * s, 'b2': jnp.zeros((DT,), jnp.float32), 'log_dt': jnp.log(0.001) + jax.random.uniform(ks[9], (DT,), jnp.float32) * (jnp.log(0.1) - jnp.log(0.001)), 'A_re': -0.5 * jnp.ones((DT, N_STATE), jnp.float32), 'A_im': jnp.tile(jnp.pi * jnp.arange(N_STATE, dtype=jnp.float32), (DT, 1)), 'C_re': jax.random.normal(ks[10], (DT, N_STATE), jnp.float32) * 0.5 ** 0.5, 'C_im': jax.random.normal(ks[11], (DT, N_STATE), jnp.float32) * 0.5 ** 0.5, 'D_skip': jax.random.normal(ks[12], (DT,), jnp.float32), 'mod_gate': jnp.array(0.5, jnp.float32)}
        return inp
    _L0_xattn_all = _L0_xattn_setup()
    _L0_xattn_in = {k: v for k, v in _L0_xattn_all.items() if k in ('Wq', 'Wk', 'Wv', 'W_film_in', 'b_film_in', 'W_film_out', 'b_film_out', 'g_norm_in', 'b_norm_in', 'g_norm_out', 'b_norm_out', 'g_ffn', 'b_ffn', 'W1', 'b1', 'W2', 'b2', 'log_dt', 'A_re', 'A_im', 'C_re', 'C_im', 'D_skip', 'mod_gate')}
    del _L0_xattn_all

    def _L0_ffn_setup():
        import jax, jax.numpy as jnp
        import numpy as np
        B, N, C, F, E, K = (2, 256, 128, 512, 8, 2)
        key = jax.random.key(seed)
        k = jax.random.split(key, 6)
        xavier1 = float(np.sqrt(6.0 / (C + F)))
        xavier2 = float(np.sqrt(6.0 / (F + C)))
        return {'x': jax.random.normal(k[0], (B, N, C), dtype=jnp.float32), 'router_w': jax.random.normal(k[1], (E, C), dtype=jnp.float32) * 0.01, 'w1': jax.random.uniform(k[2], (E, F, C), dtype=jnp.float32, minval=-xavier1, maxval=xavier1), 'b1': jnp.zeros((E, F), dtype=jnp.float32), 'w2': jax.random.uniform(k[3], (E, C, F), dtype=jnp.float32, minval=-xavier2, maxval=xavier2), 'b2': jnp.zeros((E, C), dtype=jnp.float32)}
    _L0_ffn_all = _L0_ffn_setup()
    _L0_ffn_in = {k: v for k, v in _L0_ffn_all.items() if k in ('router_w', 'w1', 'b1', 'w2', 'b2')}
    del _L0_ffn_all
    return {'x': x, 'ctx_768': ctx_768, 'mask_BxS_bf1': mask_BxS_bf1, 'mask_BxS2_bf1': mask_BxS2_bf1, 'g_xattn': g_xattn, 'g_ffn': g_ffn, 'L0_xattn_Wq': _L0_xattn_in['Wq'], 'L0_xattn_Wk': _L0_xattn_in['Wk'], 'L0_xattn_Wv': _L0_xattn_in['Wv'], 'L0_xattn_W_film_in': _L0_xattn_in['W_film_in'], 'L0_xattn_b_film_in': _L0_xattn_in['b_film_in'], 'L0_xattn_W_film_out': _L0_xattn_in['W_film_out'], 'L0_xattn_b_film_out': _L0_xattn_in['b_film_out'], 'L0_xattn_g_norm_in': _L0_xattn_in['g_norm_in'], 'L0_xattn_b_norm_in': _L0_xattn_in['b_norm_in'], 'L0_xattn_g_norm_out': _L0_xattn_in['g_norm_out'], 'L0_xattn_b_norm_out': _L0_xattn_in['b_norm_out'], 'L0_xattn_g_ffn': _L0_xattn_in['g_ffn'], 'L0_xattn_b_ffn': _L0_xattn_in['b_ffn'], 'L0_xattn_W1': _L0_xattn_in['W1'], 'L0_xattn_b1': _L0_xattn_in['b1'], 'L0_xattn_W2': _L0_xattn_in['W2'], 'L0_xattn_b2': _L0_xattn_in['b2'], 'L0_xattn_log_dt': _L0_xattn_in['log_dt'], 'L0_xattn_A_re': _L0_xattn_in['A_re'], 'L0_xattn_A_im': _L0_xattn_in['A_im'], 'L0_xattn_C_re': _L0_xattn_in['C_re'], 'L0_xattn_C_im': _L0_xattn_in['C_im'], 'L0_xattn_D_skip': _L0_xattn_in['D_skip'], 'L0_xattn_mod_gate': _L0_xattn_in['mod_gate'], 'L0_ffn_router_w': _L0_ffn_in['router_w'], 'L0_ffn_w1': _L0_ffn_in['w1'], 'L0_ffn_b1': _L0_ffn_in['b1'], 'L0_ffn_w2': _L0_ffn_in['w2'], 'L0_ffn_b2': _L0_ffn_in['b2']}

def reference(x, ctx_768, mask_BxS_bf1, mask_BxS2_bf1, g_xattn, g_ffn, L0_xattn_Wq, L0_xattn_Wk, L0_xattn_Wv, L0_xattn_W_film_in, L0_xattn_b_film_in, L0_xattn_W_film_out, L0_xattn_b_film_out, L0_xattn_g_norm_in, L0_xattn_b_norm_in, L0_xattn_g_norm_out, L0_xattn_b_norm_out, L0_xattn_g_ffn, L0_xattn_b_ffn, L0_xattn_W1, L0_xattn_b1, L0_xattn_W2, L0_xattn_b2, L0_xattn_log_dt, L0_xattn_A_re, L0_xattn_A_im, L0_xattn_C_re, L0_xattn_C_im, L0_xattn_D_skip, L0_xattn_mod_gate, L0_ffn_router_w, L0_ffn_w1, L0_ffn_b1, L0_ffn_w2, L0_ffn_b2):
    import jax
    import jax.numpy as jnp

    def _L0_xattn_ref(x_text, x_vision, text_mask, vision_mask, Wq, Wk, Wv, W_film_in, b_film_in, W_film_out, b_film_out, g_norm_in, b_norm_in, g_norm_out, b_norm_out, g_ffn, b_ffn, W1, b1, W2, b2, log_dt, A_re, A_im, C_re, C_im, D_skip, mod_gate):
        import jax, jax.numpy as jnp
        import numpy as np
        B, T, DT, G, DV = (16, 64, 128, 72, 96)
        H, DH = (4, 32)
        INNER = H * DH
        HID = 4 * DT
        N_STATE = 64
        K_TOP = 32

        def layernorm(x, g, b, eps=1e-05):
            m = x.mean(-1, keepdims=True)
            v = x.var(-1, keepdims=True)
            return (x - m) * jax.lax.rsqrt(v + eps) * g + b

        def s4d(x, log_dt, A_re, A_im, C_re, C_im, D_skip):
            Bb, L, D = x.shape
            dt = jnp.exp(log_dt)
            A = A_re + 1j * A_im
            C = C_re + 1j * C_im
            dtA = dt[:, None] * A
            dC = C * (jnp.exp(dtA) - 1.0) / A
            powers = jnp.exp(dtA[:, :, None] * jnp.arange(L))
            K = 2.0 * jnp.einsum('dn,dnl->dl', dC, powers).real
            n = 2 * L
            Kf = jnp.fft.rfft(K, n=n, axis=-1)
            xf = jnp.fft.rfft(x, n=n, axis=1)
            y = jnp.fft.irfft(xf * Kf.T[None], n=n, axis=1)[:, :L]
            return y + x * D_skip
        Bb, Tt, D = x_text.shape
        Gg = x_vision.shape[1]
        Q = (x_text @ Wq).reshape(Bb, Tt, H, DH)
        K = (x_vision @ Wk).reshape(Bb, Gg, H, DH)
        scores = jnp.einsum('bthd,bghd->bhtg', Q, K) / np.sqrt(DH).astype(np.float32)
        scores = jnp.where(vision_mask[:, None, None, :], scores, -jnp.inf)
        topv, topi = jax.lax.top_k(scores, K_TOP)
        probs = jax.nn.softmax(topv, axis=-1)
        bi = jnp.arange(Bb)[:, None, None, None]
        hi = jnp.arange(H)[None, :, None, None]
        ti = jnp.arange(Tt)[None, None, :, None]
        attn = jnp.zeros_like(scores).at[bi, hi, ti, topi].set(probs)
        attn_mean = attn.mean(axis=1)
        V = x_vision @ Wv
        c_t = jnp.einsum('btg,bgd->btd', attn_mean, V)
        c_t = c_t * text_mask[..., None]
        x = layernorm(x_text, g_norm_in, b_norm_in)
        scale_in, shift_in = jnp.split(c_t @ W_film_in + b_film_in, 2, axis=-1)
        x = x * (1.0 + mod_gate * scale_in) + mod_gate * shift_in
        y = s4d(x, log_dt, A_re, A_im, C_re, C_im, D_skip)
        scale_out, shift_out = jnp.split(c_t @ W_film_out + b_film_out, 2, axis=-1)
        y = y * (1.0 + mod_gate * scale_out) + mod_gate * shift_out
        xt = x_text + y
        h = layernorm(xt, g_ffn, b_ffn)
        h = jax.nn.gelu(h @ W1 + b1, approximate=False) @ W2 + b2
        xt = xt + h
        return layernorm(xt, g_norm_out, b_norm_out)

    def _L0_ffn_ref(x, router_w, w1, b1, w2, b2):
        import jax, jax.numpy as jnp
        import numpy as np
        B, N, C, F, E, K = (2, 256, 128, 512, 8, 2)
        Bb, Nn, Cc = x.shape
        x_flat = x.reshape(-1, Cc)
        logits = jnp.einsum('tc,ec->te', x_flat, router_w)
        probs = jax.nn.softmax(logits, axis=-1)
        top_w, top_idx = jax.lax.top_k(probs, K)
        top_w = top_w / (jnp.sum(top_w, axis=-1, keepdims=True) + 1e-09)
        h = jnp.einsum('tc,efc->tef', x_flat, w1) + b1[None]
        h = jax.nn.relu(h)
        y = jnp.einsum('tef,ecf->tec', h, w2) + b2[None]
        sel = jnp.take_along_axis(y, top_idx[:, :, None], axis=1)
        out = jnp.einsum('tkc,tk->tc', sel, top_w)
        return out.reshape(Bb, Nn, Cc)
    x = x + jnp.tanh(g_xattn[0]) * _L0_xattn_ref(_layernorm(x, axis=-1), ctx_768, mask_BxS_bf1, mask_BxS2_bf1, L0_xattn_Wq, L0_xattn_Wk, L0_xattn_Wv, L0_xattn_W_film_in, L0_xattn_b_film_in, L0_xattn_W_film_out, L0_xattn_b_film_out, L0_xattn_g_norm_in, L0_xattn_b_norm_in, L0_xattn_g_norm_out, L0_xattn_b_norm_out, L0_xattn_g_ffn, L0_xattn_b_ffn, L0_xattn_W1, L0_xattn_b1, L0_xattn_W2, L0_xattn_b2, L0_xattn_log_dt, L0_xattn_A_re, L0_xattn_A_im, L0_xattn_C_re, L0_xattn_C_im, L0_xattn_D_skip, L0_xattn_mod_gate)
    x = x + jnp.tanh(g_ffn[0]) * _L0_ffn_ref(_layernorm(x, axis=-1), L0_ffn_router_w, L0_ffn_w1, L0_ffn_b1, L0_ffn_w2, L0_ffn_b2)
    return x

_drawn_inputs = setup_inputs


def setup_inputs(seed=0):
    import zlib

    import numpy as np

    out = dict(_drawn_inputs(seed))
    spreads = {'L0_xattn_b_film_in': (0.0, 0.1),
     'L0_xattn_b_film_out': (0.0, 0.1),
     'L0_xattn_g_norm_in': (1.0, 0.2),
     'L0_xattn_b_norm_in': (0.0, 0.1),
     'L0_xattn_g_norm_out': (1.0, 0.2),
     'L0_xattn_b_norm_out': (0.0, 0.1),
     'L0_xattn_g_ffn': (1.0, 0.6),
     'L0_xattn_b_ffn': (0.0, 2.0),
     'L0_xattn_b1': (0.0, 0.328),
     'L0_xattn_b2': (0.0, 0.1),
     'L0_xattn_A_re': (-0.5, 0.2),
     'L0_ffn_b1': (0.0, 0.1),
     'L0_ffn_b2': (0.0, 0.1)}
    factors = {'ctx_768': 3.01,
     'L0_xattn_Wq': 6.656,
     'L0_xattn_Wk': 7.087,
     'L0_xattn_Wv': 2.861,
     'L0_xattn_W_film_in': 3.222,
     'L0_xattn_W_film_out': 4.105}
    for name, (base, spread) in spreads.items():
        noise = np.random.default_rng([zlib.crc32(name.encode()), seed]).standard_normal(out[name].shape)
        drawn = base * np.exp(spread * noise) if base else spread * noise
        out[name] = jnp.asarray(drawn.astype(out[name].dtype))
    for name, factor in factors.items():
        out[name] = (out[name] * factor).astype(out[name].dtype)
    return out
```

```python
from contextlib import ExitStack

import concourse.bass as bass
from concourse import mybir

F32 = mybir.dt.float32
I32 = mybir.dt.int32
U32 = mybir.dt.uint32
U8 = mybir.dt.uint8
ALU = mybir.AluOpType
ACT = mybir.ActivationFunctionType
AX = mybir.AxisListType

B, T, D = 32, 128, 128
G, DV = 77, 96
H, DH = 4, 32
HID = 512
CH = HID // 128
E = 8
NS = 64
GROUP = 4
N = B // GROUP
GT = GROUP * T
GG = GROUP * G
ROUNDS = 4
EPS = 1e-5
SCALE = 1.0 / float(DH) ** 0.5
MASKED = -1e30
PICKED = -3e38
LO, HI = 8, 16
NL = LO + HI
ROUND = 12582912.0
TWO_PI = 6.2831845
INV_TWO_PI = 0.15915494309189535


def count(i, per, k):
    return i * per + k


def wait(eng, sem, i, per, k):
    v = count(i, per, k)
    if isinstance(v, int) and v <= 0:
        return
    eng.wait_ge(sem, v)


def build(nc, t, out):
    with ExitStack() as ctx:
        def sb(name, shape, dt=F32):
            return ctx.enter_context(nc.sbuf_tensor(name, shape, dt))

        def sem(name):
            return ctx.enter_context(nc.semaphore(name))

        X = sb("X", [128, B, D])
        XL = sb("XL", [128, B, D])
        XIN = sb("XIN", [128, B, D])
        FO = sb("FO", [128, B, 2 * D])
        Y = sb("Y", [128, B, D])
        TOEP = sb("TOEP", [128, D * T])
        toep = TOEP[:, :].rearrange("s (d t) -> s d t", d=D)
        X3T = XIN[:, :, :].rearrange("p b d -> p (b d)")
        PS = ctx.enter_context(nc.psum_tensor("PS", [128, 8, 512], F32))

        Wq = sb("Wq", [D, D])
        Wk = sb("Wk", [DV, D])
        Wv = sb("Wv", [DV, D])
        WF = sb("WF", [D, 4 * D])
        film_row = sb("film_row", [1, 4 * D])
        mod = sb("mod", [128, 1])
        g_in = sb("g_in", [128, D])
        b_in = sb("b_in", [128, D])
        g_out = sb("g_out", [128, D])
        b_out = sb("b_out", [128, D])
        gates = sb("gates", [128, 2])
        text_mask = sb("text_mask", [128, B], U8)
        text_w = sb("text_w", [128, B])
        ctx_mask = sb("ctx_mask", [128, B * G], U8)
        W1 = sb("W1", [D, HID])
        W2 = sb("W2", [128, CH, D])
        b1 = sb("b1", [128, CH])
        b2row = sb("b2row", [1, D])
        g_ffn = sb("g_ffn", [D, 1])
        b_ffn = sb("b_ffn", [D, 1])
        RW = sb("RW", [D, E])
        E1b = sb("E1b", [128, E, CH])
        E2b = sb("E2b", [1, E, D])
        ident = sb("ident", [128, 128])
        anti = sb("anti", [128, 128])
        ones = sb("ones", [128, 128])
        mhalf = sb("mhalf", [128, GROUP])
        eps = sb("eps", [128, GROUP])
        idle = sb("idle", [1, 1])

        taken = 0

        def scratch(width):
            nonlocal taken
            taken += width
            assert taken <= B * D
            return Y[:, :, :].rearrange("p b d -> p (b d)")[:, taken - width:taken]

        ctx_T = sb("ctx_T", [DV, GG])
        stats = sb("stats", [128, GROUP, 6])
        mv = sb("mv", [128, GROUP, 2])
        rs = sb("rs", [128, 8, GROUP])
        xl = sb("xl", [128, GROUP, D])
        xlT = sb("xlT", [128, GT])
        QT = sb("QT", [128, GT])
        KT = sb("KT", [128, GG])
        V = sb("V", [G, GROUP, D])
        V_next = sb("V_next", [G, GROUP, D])
        bias_rows = sb("bias_rows", [128, GG])
        S = scratch(H * GROUP * G).rearrange("p (h j g) -> p h j g", h=H, j=GROUP)
        left = scratch(GROUP * G).rearrange("p (j g) -> p j g", j=GROUP)
        top = sb("top", [128, ROUNDS, GROUP, 8])
        neg_max = sb("neg_max", [128, H, GROUP])
        P = scratch(H * GROUP * G).rearrange("p (h j g) -> p h j g", h=H, j=GROUP)
        A = scratch(H * GROUP * G).rearrange("p (h j g) -> p h j g", h=H, j=GROUP)
        total = sb("total", [128, H, GROUP])
        share = sb("share", [128, H, GROUP])
        AT = sb("AT", [G, GT])
        CT = sb("CT", [128, GT])
        tmp = sb("tmp", [128, GROUP, D])

        kg = {}
        at = 0
        for name in ("are", "aim", "cre", "cim", "ldt", "dt", "re", "tu", "th", "s2", "c2", "t0", "t1", "t2",
                     "em", "q", "nr", "ni", "xr", "xi", "P", "Q"):
            kg[name] = TOEP[:, at:at + D]
            at += D
        for name, w in (("mag", NL), ("sa", NL), ("ta", NL), ("tb", LO), ("sb", LO), ("U", LO), ("u2", LO)):
            kg[name] = TOEP[:, at:at + D * w].rearrange("p (d l) -> p d l", l=w)
            at += D * w
        assert at <= D * T
        steps_i = sb("steps_i", [128, NL], I32)
        steps = sb("steps", [128, NL])
        quarter = sb("quarter", [128, 2])
        sign2 = sb("sign2", [128, 1])
        minus1 = sb("minus1", [128, D])
        kern = sb("kern", [128, 32 * HI])
        dskip = sb("dskip", [128, 32])
        zero = sb("zero", [128, 128])
        kpad = nc.dram_tensor("kpad", [D, 2 * T], F32, kind="Internal")

        S_ = {}
        for name in """loads_first loads_kernel loads_mlp loads_moe x_loaded ctx_loaded bn_done consts kg_chain kg_dve kg_act
            kg_mm kpad_written toep_loaded masks masks_clear v_moved rev rev_act rev_dve film_params stats_a rstd_a norm_a pool_a tr_a trev_a bias_ready qkv
            qkvev scores S_ready max_done repl_done neg_done exp_done sel_done sum_done share_done weights attnT
            attnTev cT cTev film fo xin conv y_ready""".split():
            S_[name] = sem(name)

        st = type("Sems", (), S_)

        def sl(i):
            return bass.ds(i * GROUP, GROUP)

        def apart(eng, i):
            if not isinstance(i, int):
                nc.vector.memset(idle[:, :], 0.0)

        PER = dict(stats=GROUP, rstd=8, norm=GROUP, pool=7, tr=1, trev=1, bias=1, qkv=3, qkvev=3, scores=H,
                   S=H, neg=H, exp=H * GROUP, sel=H, sum=H,
                   share=2, weights=1, attnT=1, attnTev=1, cT=1, cTev=1, film=GROUP, fo=GROUP, xin=2 * GROUP)

        def mean_var(eng, src, mvt, signal):
            for j in range(GROUP):
                nc.vector.bn_stats(stats[:, j, :], src(j)).then_inc(st.bn_done, 1)
            for j in range(GROUP):
                eng.wait_ge(st.bn_done, j + 1)
                nc.vector.bn_aggr(mvt[:, j, :], stats[:, j, :]).then_inc(signal, 1)
            eng.sem_clear(st.bn_done)

        def stats_a(eng, i):
            wait(eng, st.x_loaded, i, 16, 16)
            wait(eng, st.norm_a, i, GROUP, 0)
            wait(eng, st.rstd_a, i, 8, 0)
            apart(eng, i)
            mean_var(eng, lambda j: X[:, bass.ds(i * GROUP + j, 1), :], mv, st.stats_a)

        def rstd_a(eng, i):
            wait(eng, st.stats_a, i, PER["stats"], GROUP)
            wait(eng, st.norm_a, i, GROUP, 0)
            wait(eng, st.pool_a, i, PER["pool"], 0)
            mean, var = mv[:, :, 0], mv[:, :, 1]
            ve, r, nmr, vr, r2 = (rs[:, k, :] for k in range(5))
            k = 0

            def step(ins):
                nonlocal k
                k += 1
                ins.then_inc(st.rstd_a, 1)

            def last():
                wait(eng, st.rstd_a, i, 8, k)

            step(nc.gpsimd.tensor_tensor(ve, var, eps[:, :], ALU.add))
            last()
            step(nc.gpsimd.tensor_tensor(r, ve, mhalf[:, :], ALU.pow))
            last()
            step(nc.gpsimd.tensor_tensor(nmr, mean, r, ALU.mult))
            last()
            step(nc.gpsimd.tensor_tensor(nmr, nmr, minus1[:, 0:GROUP], ALU.mult))
            step(nc.gpsimd.tensor_tensor(vr, var, r, ALU.mult))
            last()
            step(nc.gpsimd.tensor_tensor(vr, vr, r, ALU.mult))
            last()
            step(nc.gpsimd.tensor_tensor(vr, vr, eps[:, :], ALU.add))
            last()
            step(nc.gpsimd.tensor_tensor(r2, vr, mhalf[:, :], ALU.pow))

        def norm_a(eng, i):
            wait(eng, st.rstd_a, i, 8, 4)
            wait(eng, st.pool_a, i, PER["pool"], 0)
            wait(eng, st.tr_a, i, 1, 0)
            for j in range(GROUP):
                nc.scalar.activation(xl[:, j, :], X[:, bass.ds(i * GROUP + j, 1), :], ACT.Identity,
                                     bias=rs[:, 2, j:j + 1], scale=rs[:, 1, j:j + 1]).then_inc(st.norm_a, 1)

        def affine_a(eng, i):
            wait(eng, st.norm_a, i, GROUP, GROUP)
            wait(eng, st.rstd_a, i, 8, 8)
            nc.gpsimd.tensor_copy(XL[:, sl(i), :], xl[:, :, :]).then_inc(st.pool_a, 1)
            for j in range(GROUP):
                nc.gpsimd.tensor_scalar(tmp[:, j, :], xl[:, j, :], rs[:, 4, j:j + 1], None,
                                        ALU.mult).then_inc(st.pool_a, 1)
            wait(eng, st.pool_a, i, PER["pool"], 1 + GROUP)
            nc.gpsimd.tensor_tensor(tmp[:, :, :], tmp[:, :, :], g_in[:, :].unsqueeze(1).to_broadcast([128, GROUP, D]),
                                    ALU.mult).then_inc(st.pool_a, 1)
            wait(eng, st.pool_a, i, PER["pool"], 2 + GROUP)
            nc.gpsimd.tensor_tensor(XIN[:, sl(i), :], tmp[:, :, :],
                                    b_in[:, :].unsqueeze(1).to_broadcast([128, GROUP, D]),
                                    ALU.add).then_inc(st.pool_a, 1)

        def bias_a(eng, i):
            wait(eng, st.scores, i, H, 0)
            nc.vector.tensor_scalar(bias_rows[0:97, :], ctx_mask[0:97, bass.ds(i * GG, GG)], -MASKED, MASKED,
                                    ALU.mult, ALU.add).then_inc(st.bias_ready, 1)

        def tr_a(eng, i):
            wait(eng, st.norm_a, i, GROUP, GROUP)
            wait(eng, st.fo, i - 2, GROUP, 0)
            wait(eng, st.xin, i - 2, PER["xin"], 0)
            wait(eng, st.qkvev, i, 3, 0)
            for j in range(GROUP):
                last = nc.tensor.transpose(PS[:, 0, j * T:(j + 1) * T], xl[:, j, :], ident[:, :])
            last.then_inc(st.tr_a, 1)

        def trev_a(eng, i):
            wait(eng, st.tr_a, i, 1, 1)
            wait(eng, st.qkv, i, 3, 0)
            nc.scalar.activation(xlT[:, :], PS[:, 0, :], ACT.Copy).then_inc(st.trev_a, 1)

        def qkv_a(eng, i):
            wait(eng, st.trev_a, i, 1, 1)
            wait(eng, st.ctx_loaded, i, 16, 16)
            nc.tensor.matmul(PS[:, 1, :], Wq[:, :], xlT[:, :], start=True, stop=True).then_inc(st.qkv, 1)
            nc.tensor.matmul(PS[:, 2, 0:GG], Wk[:, :], ctx_T[:, :], start=True, stop=True).then_inc(st.qkv, 1)
            for j in range(GROUP):
                last = nc.tensor.matmul(PS[0:G, 0, j * D:(j + 1) * D], ctx_T[:, j * G:(j + 1) * G], Wv[:, :],
                                        start=True, stop=True)
            last.then_inc(st.qkv, 1)

        def qkvev_a(eng, i):
            wait(eng, st.scores, i, H, 0)
            wait(eng, st.qkv, i, 3, 1)
            nc.scalar.activation(QT[:, :], PS[:, 1, :], ACT.Copy).then_inc(st.qkvev, 1)
            wait(eng, st.qkv, i, 3, 2)
            nc.scalar.activation(KT[:, :], PS[:, 2, 0:GG], ACT.Copy).then_inc(st.qkvev, 1)

        def vev_a(eng, i):
            wait(eng, st.qkv, i, 3, 3)
            wait(eng, st.v_moved, i, 1, 0)
            nc.scalar.activation(V_next[:, :, :].rearrange("g j d -> g (j d)"), PS[0:G, 0, :],
                                 ACT.Copy).then_inc(st.qkvev, 1)

        def v_a(eng, i):
            wait(eng, st.cT, i, 1, 0)
            wait(eng, st.qkvev, i, 3, 3)
            nc.gpsimd.tensor_tensor(V[:, :, :], V_next[:, :, :],
                                    ones[0:G, :].unsqueeze(1).to_broadcast([G, GROUP, D]), ALU.mult).then_inc(st.v_moved, 1)

        def scores_a(eng, i, h):
            if h == 0:
                wait(eng, st.qkvev, i, 3, 2)
                wait(eng, st.bias_ready, i, 1, 1)
            wait(eng, st.S_ready, i, H, h + 1 - H)
            r = slice(h * DH, (h + 1) * DH)
            o = slice(h * DH, h * DH + 1)
            nc.tensor.matmul(PS[:, 4 + h, 0:GG], ones[o, :], bias_rows[o, :], start=True, stop=False)
            for j in range(GROUP):
                last = nc.tensor.matmul(PS[:, 4 + h, j * G:(j + 1) * G], QT[r, j * T:(j + 1) * T],
                                        KT[r, j * G:(j + 1) * G], start=False, stop=j == GROUP - 1)
            last.then_inc(st.scores, 1)

        def s_a(eng, i, h):
            wait(eng, st.scores, i, H, h + 1)
            wait(eng, st.sel_done, i, H, h + 1 - H)
            wait(eng, st.exp_done, i, PER["exp"], (h + 1) * GROUP - PER["exp"])
            nc.scalar.activation(S[:, h, :, :].rearrange("p j g -> p (j g)"), PS[:, 4 + h, 0:GG], ACT.Copy,
                                 scale=SCALE).then_inc(st.S_ready, 1)

        def topk_a(eng, i, h):
            wait(eng, st.S_ready, i, H, h + 1)
            apart(eng, i)
            for r in range(ROUNDS):
                for j in range(GROUP):
                    if r:
                        eng.wait_ge(st.repl_done, (r - 1) * GROUP + j + 1)
                    src = left[:, j, :] if r else S[:, h, j, :]
                    nc.vector.max(top[:, r, j, :], src).then_inc(st.max_done, 1)
                for j in range(GROUP):
                    eng.wait_ge(st.max_done, r * GROUP + j + 1)
                    src = left[:, j, :] if r else S[:, h, j, :]
                    nc.vector.match_replace(left[:, j, :], top[:, r, j, :], src, PICKED).then_inc(st.repl_done, 1)
                if r == 0:
                    wait(eng, st.exp_done, i, PER["exp"], (h + 1) * GROUP - PER["exp"])
                    nc.vector.tensor_scalar(neg_max[:, h, :], top[:, 0, :, 0], -1.0, None,
                                            ALU.mult).then_inc(st.neg_done, 1)
            wait(eng, st.exp_done, i, PER["exp"], (h + 1) * GROUP)
            eng.wait_ge(st.repl_done, ROUNDS * GROUP)
            p, l = P[:, h, :, :], left[:, :, :]
            nc.vector.scalar_tensor_tensor(out=p, in0=l, scalar=PICKED, in1=p, op0=ALU.is_equal,
                                           op1=ALU.mult).then_inc(st.sel_done, 1)
            wait(eng, st.sel_done, i, H, h + 1)
            nc.vector.tensor_reduce(total[:, h, :], p, AX.X, ALU.add).then_inc(st.sum_done, 1)
            eng.sem_clear(st.max_done)
            eng.sem_clear(st.repl_done)

        def exp_a(eng, i, h):
            wait(eng, st.neg_done, i, H, h + 1)
            wait(eng, st.weights, i, 1, 0)
            for j in range(GROUP):
                nc.scalar.activation(P[:, h, j, :], S[:, h, j, :], ACT.Exp,
                                     bias=neg_max[:, h, j:j + 1]).then_inc(st.exp_done, 1)

        def share_a(eng, i):
            wait(eng, st.sum_done, i, H, H)
            wait(eng, st.weights, i, 1, 0)
            nc.vector.reciprocal(share[:, :, :], total[:, :, :]).then_inc(st.share_done, 1)
            wait(eng, st.share_done, i, 2, 1)
            nc.vector.tensor_tensor(share[:, :, :], share[:, :, :],
                                    text_w[:, sl(i)].unsqueeze(1).to_broadcast([128, H, GROUP]),
                                    ALU.mult).then_inc(st.share_done, 1)

        def weights_a(eng, i):
            wait(eng, st.share_done, i, 2, 2)
            wait(eng, st.attnT, i, 1, 0)
            nc.gpsimd.tensor_tensor(A[:, :, :, :].rearrange("p h j g -> p (h j) g"),
                                    P[:, :, :, :].rearrange("p h j g -> p (h j) g"),
                                    share[:, :, :].rearrange("p h j -> p (h j)").unsqueeze(2)
                                    .to_broadcast([128, H * GROUP, G]), ALU.mult).then_inc(st.weights, 1)

        def attnT_a(eng, i):
            wait(eng, st.weights, i, 1, 1)
            wait(eng, st.fo, i, GROUP, 0)
            wait(eng, st.xin, i, PER["xin"], 0)
            for j in range(GROUP):
                for h in range(H):
                    last = nc.tensor.matmul(PS[0:G, 3, j * T:(j + 1) * T], A[:, h, j, :], ident[:, :],
                                            start=h == 0, stop=h == H - 1)
            last.then_inc(st.attnT, 1)

        def attnTev_a(eng, i):
            wait(eng, st.attnT, i, 1, 1)
            wait(eng, st.cT, i, 1, 0)
            nc.scalar.activation(AT[:, :], PS[0:G, 3, :], ACT.Copy).then_inc(st.attnTev, 1)

        def cT_a(eng, i):
            wait(eng, st.attnTev, i, 1, 1)
            wait(eng, st.v_moved, i, 1, 1)
            for j in range(GROUP):
                last = nc.tensor.matmul(PS[:, 3, j * T:(j + 1) * T], V[:, j, :], AT[:, j * T:(j + 1) * T],
                                        start=True, stop=True)
            last.then_inc(st.cT, 1)

        def cTev_a(eng, i):
            wait(eng, st.cT, i, 1, 1)
            wait(eng, st.film, i, GROUP, 0)
            nc.scalar.activation(CT[:, :], PS[:, 3, :], ACT.Copy).then_inc(st.cTev, 1)

        bank_of = (1, 2, 0, 3)

        def film_a(eng, i):
            wait(eng, st.cTev, i, 1, 1)
            last = min(i + 2, N - 1) if isinstance(i, int) else i + 2
            wait(eng, st.qkvev, last, 3, 3)
            for j in range(GROUP):
                nc.tensor.matmul(PS[:, bank_of[j], :], ones[0:1, :], film_row[:, :], start=True, stop=False)
                nc.tensor.matmul(PS[:, bank_of[j], :], CT[:, j * T:(j + 1) * T], WF[:, :], start=False,
                                 stop=True).then_inc(st.film, 1)

        def fo_a(eng, i, js):
            for j in js:
                wait(eng, st.film, i, GROUP, j + 1)
                nc.scalar.activation(FO[:, bass.ds(i * GROUP + j, 1), :], PS[:, bank_of[j], 2 * D:],
                                     ACT.Copy).then_inc(st.fo, 1)

        def xin_a(eng, i, js):
            wait(eng, st.pool_a, i, PER["pool"], 3 + GROUP)
            for j in js:
                wait(eng, st.fo, i, GROUP, j + 1)
                z = XIN[:, bass.ds(i * GROUP + j, 1), :]
                nc.vector.tensor_tensor(z, z, PS[:, bank_of[j], 0:D].unsqueeze(1), ALU.mult).then_inc(st.xin, 1)
                wait(eng, st.xin, i, PER["xin"], 2 * j + 1)
                nc.vector.tensor_tensor(z, z, PS[:, bank_of[j], D:2 * D].unsqueeze(1), ALU.add).then_inc(st.xin, 1)

        def dve_a(eng, i, has_prev, has_next):
            if has_next:
                stats_a(eng, i + 1)
                bias_a(eng, i + 1)
            topk_a(eng, i, 0)
            topk_a(eng, i, 1)
            topk_a(eng, i, 2)
            if has_prev:
                xin_a(eng, i - 1, (0, 1))
            topk_a(eng, i, 3)
            share_a(eng, i)
            if has_prev:
                xin_a(eng, i - 1, (2, 3))

        def pool_a(eng, i, has_prev, has_next):
            if has_next:
                rstd_a(eng, i + 1)
                affine_a(eng, i + 1)
            v_a(eng, i)
            weights_a(eng, i)

        def act_a(eng, i, has_prev, has_next):
            if has_next:
                norm_a(eng, i + 1)
            exp_a(eng, i, 0)
            s_a(eng, i, 3)
            if has_next:
                trev_a(eng, i + 1)
            exp_a(eng, i, 1)
            if has_prev:
                attnTev_a(eng, i - 1)
            if has_next:
                qkvev_a(eng, i + 1)
            exp_a(eng, i, 2)
            if has_prev:
                cTev_a(eng, i - 1)
            if has_next:
                vev_a(eng, i + 1)
                s_a(eng, i + 1, 0)
            if has_prev:
                fo_a(eng, i - 1, (0, 1))
            exp_a(eng, i, 3)
            if has_next:
                s_a(eng, i + 1, 1)
                s_a(eng, i + 1, 2)
            if has_prev:
                fo_a(eng, i - 1, (2, 3))

        def pe_a(eng, i, has_prev, has_next):
            if has_next:
                tr_a(eng, i + 1)
            if has_prev:
                attnT_a(eng, i - 1)
            if has_next:
                qkv_a(eng, i + 1)
            if has_prev:
                cT_a(eng, i - 1)
            if has_next:
                for h in range(H):
                    scores_a(eng, i + 1, h)
            if has_prev:
                film_a(eng, i - 1)

        def steps_of(eng, body, after_first=None):
            body(eng, 0, False, True)
            if after_first:
                after_first()
            with eng.Fori(1, N - 1) as i:
                body(eng, i, True, True)
            body(eng, N - 1, True, False)

        late_at = 3 * E * HID

        def late(width):
            nonlocal late_at
            late_at += width
            assert late_at <= D * T
            return TOEP[:, late_at - width:late_at]

        hs, hT, x2n, x3T = tmp, xlT, xl, QT
        x3 = late(GROUP * D).rearrange("p (j d) -> p j d", j=GROUP)
        hid = late(CH * GT).rearrange("p (c t) -> p c t", c=CH)
        b1p = sb("b1p", [128, CH])
        W1g = sb("W1g", [D, HID])
        mv1, mv2, mv3 = sb("mv1", [128, GROUP, 2]), sb("mv2", [128, GROUP, 2]), sb("mv3", [128, GROUP, 2])
        rs1, rs2, rs3 = sb("rs1", [128, 3, GROUP]), sb("rs2", [128, 3, GROUP]), sb("rs3", [128, 3, GROUP])
        logits = late(B * E).rearrange("p (b e) -> p b e", e=E)
        for name in """prep_pe prep_act prep_pool xt s1 r1 n1 tr1 tr1ev up act down xt2 s2 r2 n2 xb x1 s3 r3 n3 tr3 tr3ev x3keep
            route logit""".split():
            S_[name] = sem(name)
        st2 = type("Sems2", (), S_)

        def norm_stats(eng, i, src, mvt, signal):
            apart(eng, i)
            mean_var(eng, src, mvt, signal)

        def norm_factors(eng, i, mvt, rst, have, signal, used):
            wait(eng, have, i, GROUP, GROUP)
            wait(eng, used, i, GROUP, 0)
            nc.gpsimd.tensor_tensor(rst[:, 0, :], mvt[:, :, 1], eps[:, :], ALU.add).then_inc(signal, 1)
            wait(eng, signal, i, 4, 1)
            nc.gpsimd.tensor_tensor(rst[:, 1, :], rst[:, 0, :], mhalf[:, :], ALU.pow).then_inc(signal, 1)
            wait(eng, signal, i, 4, 2)
            nc.gpsimd.tensor_tensor(rst[:, 2, :], mvt[:, :, 0], rst[:, 1, :], ALU.mult).then_inc(signal, 1)
            wait(eng, signal, i, 4, 3)
            nc.gpsimd.tensor_tensor(rst[:, 2, :], rst[:, 2, :], minus1[:, 0:GROUP], ALU.mult).then_inc(signal, 1)

        def normalise(eng, i, dst, src, rst, have, signal):
            wait(eng, have, i, 4, 4)
            for j in range(GROUP):
                nc.scalar.activation(dst(j), src(j), ACT.Identity, bias=rst[:, 2, j:j + 1],
                                     scale=rst[:, 1, j:j + 1]).then_inc(signal, 1)

        def row(arr, i, j):
            return arr[:, bass.ds(i * GROUP + j, 1), :]

        def xt_b(eng, i):
            y = Y[:, sl(i), :]
            if isinstance(i, int) and i == 0:
                eng.wait_ge(st.y_ready, 8)
            nc.vector.tensor_tensor(y, y, FO[:, sl(i), 0:D], ALU.mult).then_inc(st2.xt, 1)
            wait(eng, st2.xt, i, 3, 1)
            nc.vector.tensor_tensor(y, y, FO[:, sl(i), D:2 * D], ALU.add).then_inc(st2.xt, 1)
            wait(eng, st2.xt, i, 3, 2)
            nc.vector.tensor_tensor(y, y, XL[:, sl(i), :], ALU.add).then_inc(st2.xt, 1)
            wait(eng, st2.xt, i, 3, 3)
            wait(eng, st2.r1, i, 4, 0)
            norm_stats(eng, i, lambda j: row(Y, i, j), mv1, st2.s1)

        def n1_b(eng, i):
            wait(eng, st2.tr1, i, 1, 0)
            normalise(eng, i, lambda j: hs[:, j, :], lambda j: row(Y, i, j), rs1, st2.r1, st2.n1)

        def tr1_b(eng, i):
            wait(eng, st2.n1, i, GROUP, GROUP)
            wait(eng, st2.tr1ev, i, 1, 0)
            for j in range(GROUP):
                last = nc.tensor.transpose(PS[:, 0, j * T:(j + 1) * T], hs[:, j, :], ident[:, :])
            last.then_inc(st2.tr1, 1)

        def tr1ev_b(eng, i):
            wait(eng, st2.tr1, i, 1, 1)
            wait(eng, st2.up, i, CH, 0)
            nc.scalar.activation(hT[:, :], PS[:, 0, :], ACT.Copy).then_inc(st2.tr1ev, 1)

        def up_b(eng, i):
            wait(eng, st2.tr1ev, i, 1, 1)
            for c in range(CH):
                wait(eng, st2.act, i, CH, c + 1 - CH)
                nc.tensor.matmul(PS[:, 1 + c, :], W1g[:, c * 128:(c + 1) * 128], hT[:, :], start=True,
                                 stop=True).then_inc(st2.up, 1)

        def gelu_b(eng, i):
            wait(eng, st2.down, i, 1, 0)
            for c in range(CH):
                wait(eng, st2.up, i, CH, c + 1)
                nc.scalar.activation(hid[:, c, :], PS[:, 1 + c, :], ACT.Gelu, bias=b1p[:, c:c + 1]).then_inc(st2.act, 1)

        def down_b(eng, i):
            wait(eng, st2.act, i, CH, CH)
            wait(eng, st2.xt2, i, 1, 0)
            for j in range(GROUP):
                o = PS[:, 5, j * D:(j + 1) * D]
                nc.tensor.matmul(o, ones[0:1, :], b2row[:, :], start=True, stop=False)
                for c in range(CH):
                    last = nc.tensor.matmul(o, hid[:, c, j * T:(j + 1) * T], W2[:, c, :], start=False, stop=c == CH - 1)
            last.then_inc(st2.down, 1)

        def xt2_b(eng, i):
            wait(eng, st2.down, i, 1, 1)
            wait(eng, st2.n1, i, GROUP, GROUP)
            y = Y[:, sl(i), :]
            nc.vector.tensor_tensor(y, y, PS[:, 5, :].rearrange("p (j d) -> p j d", j=GROUP),
                                    ALU.add).then_inc(st2.xt2, 1)
            wait(eng, st2.xt2, i, 1, 1)
            wait(eng, st2.r2, i, 4, 0)
            norm_stats(eng, i, lambda j: row(Y, i, j), mv2, st2.s2)

        def n2_b(eng, i):
            wait(eng, st2.x1, i, 2, 0)
            normalise(eng, i, lambda j: x2n[:, j, :], lambda j: row(Y, i, j), rs2, st2.r2, st2.n2)

        def xb_b(eng, i):
            nc.gpsimd.tensor_tensor(X[:, sl(i), :], X[:, sl(i), :],
                                    b_out[:, :].unsqueeze(1).to_broadcast([128, GROUP, D]), ALU.add).then_inc(st2.xb, 1)

        def x1_b(eng, i):
            wait(eng, st2.n2, i, GROUP, GROUP)
            wait(eng, st2.xb, i, 1, 1)
            nc.vector.tensor_tensor(x2n[:, :, :], x2n[:, :, :], g_out[:, :].unsqueeze(1).to_broadcast([128, GROUP, D]),
                                    ALU.mult).then_inc(st2.x1, 1)
            wait(eng, st2.x1, i, 2, 1)
            nc.vector.tensor_tensor(X[:, sl(i), :], X[:, sl(i), :], x2n[:, :, :], ALU.add).then_inc(st2.x1, 1)
            wait(eng, st2.x1, i, 2, 2)
            wait(eng, st2.r3, i, 4, 0)
            norm_stats(eng, i, lambda j: row(X, i, j), mv3, st2.s3)

        def n3_b(eng, i):
            wait(eng, st2.tr3, i, 1, 0)
            normalise(eng, i, lambda j: x3[:, j, :], lambda j: row(X, i, j), rs3, st2.r3, st2.n3)

        def tr3_b(eng, i):
            wait(eng, st2.n3, i, GROUP, GROUP)
            wait(eng, st2.tr3ev, i, 1, 0)
            for j in range(GROUP):
                last = nc.tensor.transpose(PS[:, 6, j * T:(j + 1) * T], x3[:, j, :], ident[:, :])
            last.then_inc(st2.tr3, 1)

        def tr3ev_b(eng, i):
            wait(eng, st2.tr3, i, 1, 1)
            wait(eng, st2.x3keep, i, 1, 0)
            wait(eng, st2.route, i, 1, 0)
            nc.scalar.activation(x3T[:, :], PS[:, 6, :], ACT.Copy).then_inc(st2.tr3ev, 1)

        def keep_b(eng, i):
            wait(eng, st2.tr3ev, i, 1, 1)
            nc.gpsimd.tensor_copy(X3T[:, bass.ds(i * GT, GT)], x3T[:, :]).then_inc(st2.x3keep, 1)

        def route_b(eng, i):
            wait(eng, st2.tr3ev, i, 1, 1)
            wait(eng, st2.logit, i, 1, 0)
            for j in range(GROUP):
                last = nc.tensor.matmul(PS[:, 7, j * E:(j + 1) * E], x3T[:, j * T:(j + 1) * T], RW[:, :], start=True,
                                        stop=True)
            last.then_inc(st2.route, 1)

        def logit_b(eng, i):
            wait(eng, st2.route, i, 1, 1)
            nc.vector.tensor_copy(logits[:, sl(i), :], PS[:, 7, 0:GROUP * E].rearrange("p (j e) -> p j e", e=E)
                                  ).then_inc(st2.logit, 1)

        def dve_b(eng, i, has_prev, has_next):
            if has_next:
                xt_b(eng, i + 1)
            if has_prev:
                x1_b(eng, i - 1)
            xt2_b(eng, i)
            if has_prev:
                logit_b(eng, i - 1)

        def pool_b(eng, i, has_prev, has_next):
            if has_next:
                norm_factors(eng, i + 1, mv1, rs1, st2.s1, st2.r1, st2.n1)
            if has_prev:
                norm_factors(eng, i - 1, mv3, rs3, st2.s3, st2.r3, st2.n3)
                keep_b(eng, i - 1)
            xb_b(eng, i)
            norm_factors(eng, i, mv2, rs2, st2.s2, st2.r2, st2.n2)

        def act_b(eng, i, has_prev, has_next):
            if has_prev:
                n2_b(eng, i - 1)
            if has_next:
                n1_b(eng, i + 1)
            gelu_b(eng, i)
            if has_prev:
                n3_b(eng, i - 1)
            if has_next:
                tr1ev_b(eng, i + 1)
            if has_prev:
                tr3ev_b(eng, i - 1)

        def pe_b(eng, i, has_prev, has_next):
            up_b(eng, i)
            if has_next:
                tr1_b(eng, i + 1)
            down_b(eng, i)
            if has_prev:
                tr3_b(eng, i - 1)
                route_b(eng, i - 1)

        E1 = TOEP[:, 0:E * HID].rearrange("p (e f) -> p e f", e=E)
        E2 = TOEP[:, E * HID:2 * E * HID].rearrange("p (e c d) -> p e c d", e=E, c=CH)
        ehid = TOEP[:, 2 * E * HID:2 * E * HID + 2 * CH * GT].rearrange("p (s c t) -> p s c t", s=2, c=CH)
        gate = late(B * E).rearrange("p (b e) -> p b e", e=E)
        gw = sb("gw", [128, 6, B])
        gx = late(2 * B * E).rearrange("p (k b e) -> p k b e", k=2, e=E)
        m8 = late(B * 8).rearrange("p (b e) -> p b e", e=8)
        i8 = late(B * 8).bitcast(U32).rearrange("p (b e) -> p b e", e=8)
        i8f = sb("i8f", [128, B, 2])
        eid_i = sb("eid_i", [128, E], I32)
        eid = sb("eid", [128, E])
        for name in "gate_dve gate_act eup ehid edown eacc stored".split():
            S_[name] = sem(name)
        st3 = type("Sems3", (), S_)

        def gating_dve(eng):
            n = 0

            def link(ins):
                nonlocal n
                n += 1
                ins.then_inc(st3.gate_dve, 1)
                eng.wait_ge(st3.gate_dve, n)

            for b in range(B):
                nc.vector.max(m8[:, b, :], logits[:, b, :]).then_inc(st3.gate_dve, 1)
            eng.wait_ge(st3.gate_dve, B)
            for b in range(B):
                nc.vector.max_index(i8[:, b, :], m8[:, b, :], logits[:, b, :]).then_inc(st3.gate_dve, 1)
            n = 2 * B
            eng.wait_ge(st3.gate_dve, n)
            link(nc.vector.tensor_copy(i8f[:, :, :], i8[:, :, 0:2]))
            link(nc.vector.tensor_tensor(gx[:, 0, :, :], logits[:, :, :], m8[:, :, 0:1].to_broadcast([128, B, E]),
                                         ALU.subtract))
            link(nc.vector.tensor_tensor(gw[:, 0, :], m8[:, :, 1], m8[:, :, 0], ALU.subtract))
            eng.wait_ge(st3.gate_act, 2)
            link(nc.vector.tensor_reduce(gw[:, 2, :], gx[:, 1, :, :], AX.X, ALU.add))
            link(nc.vector.scalar_tensor_tensor(out=gw[:, 3, :], in0=gw[:, 2, :], scalar=1e-9, in1=gw[:, 1, :],
                                                op0=ALU.mult, op1=ALU.add))
            link(nc.vector.tensor_scalar(gw[:, 3, :], gw[:, 3, :], 1.0, None, ALU.add))
            link(nc.vector.reciprocal(gw[:, 4, :], gw[:, 3, :]))
            link(nc.vector.tensor_scalar(gw[:, 4, :], gw[:, 4, :], gates[:, 1:2], None, ALU.mult))
            link(nc.vector.tensor_tensor(gw[:, 5, :], gw[:, 4, :], gw[:, 1, :], ALU.mult))
            ids = eid[:, :].unsqueeze(1).to_broadcast([128, B, E])
            for k in range(2):
                link(nc.vector.tensor_tensor(gx[:, k, :, :], ids, i8f[:, :, k:k + 1].to_broadcast([128, B, E]),
                                             ALU.is_equal))
                link(nc.vector.tensor_tensor(gx[:, k, :, :], gx[:, k, :, :],
                                             gw[:, 4 + k, :].unsqueeze(2).to_broadcast([128, B, E]), ALU.mult))
            link(nc.vector.tensor_tensor(gate[:, :, :], gx[:, 0, :, :], gx[:, 1, :, :], ALU.add))

        def gating_act(eng):
            eng.wait_ge(st3.gate_dve, 2 * B + 3)
            nc.scalar.activation(gx[:, 1, :, :], gx[:, 0, :, :], ACT.Exp).then_inc(st3.gate_act, 1)
            nc.scalar.activation(gw[:, 1, :], gw[:, 0, :], ACT.Exp).then_inc(st3.gate_act, 1)

        def eup_c(eng, i, e):
            for c in range(CH):
                wait(eng, st3.ehid_act if c % 2 == 0 else st3.ehid_dve, i, 2 * E, max(0, 2 * (e - 1) + c // 2 + 1))
                nc.tensor.matmul(PS[:, c, :], E1[:, e, c * 128:(c + 1) * 128], X3T[:, bass.ds(i * GT, GT)],
                                 start=True, stop=True).then_inc(st3.eup, 1)

        def edown_c(eng, i, e):
            wait(eng, st3.ehid_act, i, 2 * E, 2 * e + 2)
            wait(eng, st3.ehid_dve, i, 2 * E, 2 * e + 2)
            wait(eng, st3.eacc, i, GROUP * E, max(0, GROUP * (e - 1)))
            for j in range(GROUP):
                o = PS[:, 4 + e % 2, j * D:(j + 1) * D]
                nc.tensor.matmul(o, ones[0:1, :], E2b[:, e, :], start=True, stop=False)
                for c in range(CH):
                    last = nc.tensor.matmul(o, ehid[:, e % 2, c, j * T:(j + 1) * T], E2[:, e, c, :], start=False,
                                            stop=c == CH - 1)
            last.then_inc(st3.edown, 1)

        S_["ehid_act"], S_["ehid_dve"] = sem("ehid_act"), sem("ehid_dve")
        st3 = type("Sems3", (), S_)

        def relu_act(eng, i, e):
            wait(eng, st3.edown, i, E, max(0, e - 1))
            for c in range(0, CH, 2):
                wait(eng, st3.eup, i, CH * E, CH * e + c + 1)
                nc.scalar.activation(ehid[:, e % 2, c, :], PS[:, c, :], ACT.Relu,
                                     bias=E1b[:, e, c:c + 1]).then_inc(st3.ehid_act, 1)

        def relu_dve(eng, i, e):
            wait(eng, st3.edown, i, E, max(0, e - 1))
            for c in range(1, CH, 2):
                wait(eng, st3.eup, i, CH * E, CH * e + c + 1)
                nc.vector.tensor_scalar(ehid[:, e % 2, c, :], PS[:, c, :], E1b[:, e, c:c + 1], 0.0, ALU.add,
                                        ALU.max).then_inc(st3.ehid_dve, 1)

        def acc_dve(eng, i, e):
            wait(eng, st3.edown, i, E, e + 1)
            wait(eng, st3.eacc, i, GROUP * E, GROUP * e)
            for j in range(GROUP):
                x = X[:, bass.ds(i * GROUP + j, 1), :]
                nc.vector.scalar_tensor_tensor(out=x, in0=PS[:, 4 + e % 2, j * D:(j + 1) * D].unsqueeze(1),
                                               scalar=gate[:, bass.ds(i * GROUP + j, 1), e], in1=x,
                                               op0=ALU.mult, op1=ALU.add).then_inc(st3.eacc, 1)

        kpad_ap = kpad.ap()
        KG_DVE = 8
        KG_CHAIN = 54
        block = ctx.enter_context(nc.Block())

        @block.sync
        def _(sp):
            for src, dst in ((t["Wq"], Wq[:, :]), (t["Wk"], Wk[:, :]), (t["Wv"], Wv[:, :])):
                sp.dma_start(dst, src).then_inc(st.loads_first, 16)
            sp.wait_ge(st.masks_clear, 1)
            for h in range(H):
                sp.dma_start(ctx_mask[h * DH:h * DH + 1, :], t["ctx_mask"]).then_inc(st.loads_first, 16)
            sp.dma_start(text_mask[:, :], t["text_mask"]).then_inc(st.loads_first, 16)
            for dst, src in ((g_in, t["g_in"]), (b_in, t["b_in"]), (mod, t["mod"])):
                sp.dma_start(dst[:, :], src.to_broadcast([128, src.shape[1]])).then_inc(st.loads_first, 16)
            for k, name in enumerate(("WFi", "WFo")):
                sp.dma_start(WF[:, k * 256:(k + 1) * 256], t[name]).then_inc(st.loads_first, 16)
            for k, name in enumerate(("bFi", "bFo")):
                sp.dma_start(film_row[:, k * 256:(k + 1) * 256], t[name]).then_inc(st.loads_first, 16)
            def load(i):
                wait(sp, st.x_loaded, i, 16, 0)
                sp.dma_start(X[:, sl(i), :], t["x"][:, sl(i), :]).then_inc(st.x_loaded, 16)
                wait(sp, st.qkv, i, 3, 0)
                sp.dma_start(ctx_T[:, :], t["ctx"][:, bass.ds(i * GG, GG)]).then_inc(st.ctx_loaded, 16)
            for i in range(3):
                load(i)
            sp.wait_ge(st.consts, 9)
            sp.dma_start(kpad_ap[:, 0:T - 1], zero[:, 0:T - 1]).then_inc(st.kpad_written, 16)
            sp.wait_ge(st.kg_dve, KG_DVE)
            for q in range(4):
                sp.dma_start(bass.AP(tensor=kpad, offset=T - 1 + 32 * q * 2 * T, ap=[[HI, LO], [2 * T, 32], [1, HI]]),
                             kern[32 * q:32 * q + LO, :].rearrange("a (d b) -> a d b", b=HI)
                             ).then_inc(st.kpad_written, 16)
            sp.wait_ge(st.kpad_written, 16 * 5)
            for q in range(8):
                c = D // 8
                sp.dma_start(toep[:, q * c:(q + 1) * c, :],
                             bass.AP(tensor=kpad, offset=q * c * 2 * T, ap=[[1, T], [2 * T, c], [1, T]])
                             ).then_inc(st.toep_loaded, 16)
            with sp.Fori(3, N) as i:
                load(i)
            sp.wait_ge(st.conv, 8)
            sp.dma_start(E1, t["E1"]).then_inc(st.loads_moe, 16)
            for e in range(E):
                sp.dma_start(E2[:, e, :, :], t["E2"][:, e, :, :]).then_inc(st.loads_moe, 16)
            with sp.Fori(0, N) as i:
                wait(sp, st3.eacc, i, GROUP * E, GROUP * E)
                sp.dma_start(out[:, sl(i), :], X[:, sl(i), :]).then_inc(st3.stored, 16)
            sp.wait_ge(st3.stored, 16 * N)

        @block.gpsimd
        def _(pool):
            nc.gpsimd.memset(ident[:, :], 0.0).then_inc(st.consts, 1)
            nc.gpsimd.memset(ones[:, :], 1.0).then_inc(st.consts, 1)
            nc.gpsimd.memset(mhalf[:, :], -0.5).then_inc(st.consts, 1)
            nc.gpsimd.memset(zero[:, :], 0.0).then_inc(st.consts, 1)
            nc.gpsimd.memset(eps[:, :], EPS).then_inc(st.consts, 1)
            nc.gpsimd.memset(anti[:, :], 0.0).then_inc(st.consts, 1)
            nc.gpsimd.iota(steps_i[:, 0:LO], [[HI, LO]], base=0, channel_multiplier=0).then_inc(st.consts, 1)
            nc.gpsimd.iota(steps_i[:, LO:NL], [[1, HI]], base=0, channel_multiplier=0).then_inc(st.consts, 1)
            nc.gpsimd.iota(eid_i[:, :], [[1, E]], base=0, channel_multiplier=0).then_inc(st.consts, 1)
            pool.wait_ge(st.consts, 9)
            nc.gpsimd.affine_select(out=ident[:, :], in_=ident[:, :], compare_op=ALU.not_equal, fill=1.0, base=0,
                                    pattern=[[-1, 128]], channel_multiplier=1).then_inc(st.consts, 1)
            nc.gpsimd.affine_select(out=anti[:, :], in_=anti[:, :], compare_op=ALU.not_equal, fill=1.0, base=-127,
                                    pattern=[[1, 128]], channel_multiplier=1).then_inc(st.consts, 1)
            nc.gpsimd.tensor_copy(steps[:, :], steps_i[:, :]).then_inc(st.consts, 1)
            nc.gpsimd.tensor_copy(eid[:, :], eid_i[:, :]).then_inc(st.consts, 1)
            pool.wait_ge(st.consts, 13)
            pool.wait_ge(st.masks, 7)
            rstd_a(pool, 0)
            pool.wait_ge(st.loads_first, 16 * 15)
            affine_a(pool, 0)
            steps_of(pool, pool_a)
            norm_factors(pool, 0, mv1, rs1, st2.s1, st2.r1, st2.n1)
            pool.wait_ge(st2.prep_pool, 4)
            steps_of(pool, pool_b)
            norm_factors(pool, N - 1, mv3, rs3, st2.s3, st2.r3, st2.n3)
            keep_b(pool, N - 1)

        @block.scalar
        def _(act):
            for dst, src in ((kg["are"], "are"), (kg["aim"], "aim"), (kg["cre"], "cre"), (kg["cim"], "cim")):
                for half in range(2):
                    act.dma_start(dst[half * NS:(half + 1) * NS, :], t[src]).then_inc(st.loads_kernel, 16)
            act.dma_start(kg["ldt"], t["ldt"].to_broadcast([128, D])).then_inc(st.loads_kernel, 16)
            act.wait_ge(st.masks_clear, 2)
            for q in range(4):
                act.dma_start(dskip[32 * q:32 * q + 1, :], t["dskip"][:, 32 * q:32 * q + 32]).then_inc(st.loads_kernel, 16)
            act.dma_start(W1[:, :], t["W1"]).then_inc(st.loads_mlp, 16)
            act.dma_start(W2[:, :, :], t["W2"]).then_inc(st.loads_mlp, 16)
            act.dma_start(b1[:, :], t["b1"]).then_inc(st.loads_mlp, 16)
            act.dma_start(b2row[:, :], t["b2"]).then_inc(st.loads_mlp, 16)
            act.dma_start(g_ffn[:, :], t["g_ffn"]).then_inc(st.loads_mlp, 16)
            act.dma_start(b_ffn[:, :], t["b_ffn"]).then_inc(st.loads_mlp, 16)
            act.dma_start(RW[:, :], t["RW"]).then_inc(st.loads_mlp, 16)
            act.dma_start(E1b[:, :, :], t["E1b"]).then_inc(st.loads_mlp, 16)
            act.dma_start(E2b[:, :, :].rearrange("p e d -> p (e d)"), t["E2b"]).then_inc(st.loads_mlp, 16)
            for k, (dst, src) in enumerate(((g_out[:, :], "g_out"), (b_out[:, :], "b_out"), (gates[:, 0:1], "gx"),
                                            (gates[:, 1:2], "gf"))):
                act.dma_start(dst, t[src].to_broadcast([128, t[src].shape[1]])).then_inc(st.loads_mlp, 16)
            act.wait_ge(st.loads_kernel, 16 * 13)
            nc.scalar.activation(kg["dt"], kg["ldt"], ACT.Exp).then_inc(st.kg_act, 1)
            norm_a(act, 0)
            trev_a(act, 0)
            qkvev_a(act, 0)
            vev_a(act, 0)
            act.wait_ge(st.kg_chain, 1)
            nc.scalar.activation(kg["th"], kg["re"], ACT.Tanh, scale=0.5).then_inc(st.kg_act, 1)
            act.wait_ge(st.kg_chain, 10)
            nc.scalar.activation(kg["mag"], kg["mag"], ACT.Exp).then_inc(st.kg_act, 1)
            act.wait_ge(st.kg_chain, 17)
            nc.scalar.activation(kg["s2"], kg["s2"], ACT.Sin, scale=TWO_PI).then_inc(st.kg_act, 1)
            nc.scalar.activation(kg["c2"], kg["c2"], ACT.Sin, scale=TWO_PI).then_inc(st.kg_act, 1)
            nc.scalar.activation(kg["sa"], kg["sa"], ACT.Sin, scale=TWO_PI).then_inc(st.kg_act, 1)
            nc.scalar.activation(kg["sb"], kg["sb"], ACT.Sin, scale=TWO_PI).then_inc(st.kg_act, 1)
            for h in range(3):
                s_a(act, 0, h)
            steps_of(act, act_a)
            attnTev_a(act, N - 1)
            cTev_a(act, N - 1)
            fo_a(act, N - 1, range(GROUP))
            act.wait_ge(st.loads_mlp, 16 * 13)
            nc.scalar.activation(W1g[:, :], W1[:, :], ACT.Copy, scale=g_ffn[:, :]).then_inc(st2.prep_act, 1)
            nc.scalar.activation(gates[:, :], gates[:, :], ACT.Tanh).then_inc(st2.prep_act, 1)
            for g in range(0, N, 2):
                act.wait_ge(st.rev, g + 1)
                nc.scalar.activation(XIN[:, g * GROUP:(g + 1) * GROUP, :], PS[:, g, :].rearrange(
                    "p (j d) -> p j d", j=GROUP), ACT.Copy).then_inc(st.rev_act, 1)
            for q in range(0, 8, 2):
                act.wait_ge(st.conv, q + 1)
                nc.scalar.activation(Y[:, :, 16 * q:16 * q + 16], PS[:, q, :].rearrange("p (d b) -> p b d", b=B),
                                     ACT.Copy).then_inc(st.y_ready, 1)
            n1_b(act, 0)
            tr1ev_b(act, 0)
            steps_of(act, act_b)
            n2_b(act, N - 1)
            n3_b(act, N - 1)
            tr3ev_b(act, N - 1)
            gating_act(act)
            with act.Fori(0, N) as i:
                for e in range(E):
                    relu_act(act, i, e)

        @block.vector
        def _(dve):
            nc.vector.memset(ctx_mask[:, :], 0).then_inc(st.masks_clear, 1)
            nc.vector.memset(dskip[:, :], 0.0).then_inc(st.masks_clear, 1)
            nc.vector.memset(minus1[:, :], -1.0).then_inc(st.masks, 1)
            for p, first, second, two in ((0, 0.25, 0.0, 2.0), (64, 0.0, 0.25, -2.0)):
                nc.vector.memset(quarter[p:p + 64, 0:1], first).then_inc(st.masks, 1)
                nc.vector.memset(quarter[p:p + 64, 1:2], second).then_inc(st.masks, 1)
                nc.vector.memset(sign2[p:p + 64, :], two).then_inc(st.masks, 1)
            stats_a(dve, 0)
            dve.wait_ge(st.loads_first, 16 * 15)
            nc.vector.tensor_scalar(text_w[:, :], text_mask[:, :], 1.0 / H, None, ALU.mult).then_inc(st.masks, 1)
            bias_a(dve, 0)
            nc.vector.tensor_scalar(WF[:, :], WF[:, :], mod[:, :], None, ALU.mult).then_inc(st.film_params, 1)
            nc.vector.tensor_scalar(film_row[:, :], film_row[:, :], mod[0:1, :], None, ALU.mult).then_inc(st.film_params, 1)
            dve.wait_ge(st.film_params, 2)
            for k in range(2):
                r = film_row[:, 2 * k * D:(2 * k + 1) * D]
                nc.vector.tensor_scalar(r, r, 1.0, None, ALU.add).then_inc(st.film_params, 1)
            n = 0

            def link(ins):
                nonlocal n
                n += 1
                ins.then_inc(st.kg_chain, 1)
                dve.wait_ge(st.kg_chain, n)

            def tt(o, a, b, op):
                link(nc.vector.tensor_tensor(kg[o], kg[a], kg[b], op))

            def ts(o, a, s1, op1, s2=None, op2=ALU.bypass):
                link(nc.vector.tensor_scalar(kg[o], kg[a], s1, s2, op1, op2))

            dve.wait_ge(st.consts, 13)
            dve.wait_ge(st.loads_kernel, 16 * 13)
            dve.wait_ge(st.kg_act, 1)
            tt("re", "are", "dt", ALU.mult)
            tt("t0", "aim", "dt", ALU.mult)
            ts("tu", "t0", INV_TWO_PI, ALU.mult)
            ts("t0", "tu", 0.5, ALU.mult)
            ts("t1", "t0", ROUND, ALU.add, -ROUND, ALU.add)
            tt("s2", "t0", "t1", ALU.subtract)
            ts("t0", "t0", 0.25, ALU.add)
            ts("t1", "t0", ROUND, ALU.add, -ROUND, ALU.add)
            tt("c2", "t0", "t1", ALU.subtract)
            assert n == 9
            stp = steps[:, :].unsqueeze(1).to_broadcast([128, D, NL])
            link(nc.vector.tensor_tensor(kg["mag"], kg["re"].unsqueeze(2).to_broadcast([128, D, NL]), stp, ALU.mult))
            link(nc.vector.tensor_tensor(kg["sa"], kg["tu"].unsqueeze(2).to_broadcast([128, D, NL]), stp, ALU.mult))
            link(nc.vector.tensor_scalar(kg["tb"], kg["sa"][:, :, 0:LO], quarter[:, 1:2], None, ALU.add))
            link(nc.vector.tensor_scalar(kg["sa"], kg["sa"], quarter[:, 0:1], None, ALU.add))
            link(nc.vector.tensor_scalar(kg["ta"], kg["sa"], ROUND, -ROUND, ALU.add, ALU.add))
            link(nc.vector.tensor_tensor(kg["sa"], kg["sa"], kg["ta"], ALU.subtract))
            link(nc.vector.tensor_scalar(kg["sb"], kg["tb"], ROUND, -ROUND, ALU.add, ALU.add))
            link(nc.vector.tensor_tensor(kg["sb"], kg["tb"], kg["sb"], ALU.subtract))
            assert n == 17
            dve.wait_ge(st.kg_act, 7)
            ts("t0", "th", -1.0, ALU.mult, 1.0, ALU.add)
            link(nc.vector.reciprocal(kg["t0"], kg["t0"]))
            tt("em", "th", "t0", ALU.mult)
            ts("em", "em", 2.0, ALU.mult)
            tt("q", "s2", "s2", ALU.mult)
            ts("q", "q", 2.0, ALU.mult)
            ts("t0", "q", -1.0, ALU.mult, 1.0, ALU.add)
            tt("t0", "em", "t0", ALU.mult)
            tt("nr", "t0", "q", ALU.subtract)
            tt("t1", "s2", "c2", ALU.mult)
            ts("t0", "em", 1.0, ALU.add, 2.0, ALU.mult)
            tt("ni", "t0", "t1", ALU.mult)
            tt("t0", "cre", "nr", ALU.mult)
            tt("t1", "cim", "ni", ALU.mult)
            tt("xr", "t0", "t1", ALU.subtract)
            tt("t0", "cre", "ni", ALU.mult)
            tt("t1", "cim", "nr", ALU.mult)
            tt("xi", "t0", "t1", ALU.add)
            tt("t0", "are", "are", ALU.mult)
            tt("t1", "aim", "aim", ALU.mult)
            tt("t0", "t0", "t1", ALU.add)
            link(nc.vector.reciprocal(kg["t2"], kg["t0"]))
            tt("t0", "xr", "are", ALU.mult)
            tt("t1", "xi", "aim", ALU.mult)
            tt("t0", "t0", "t1", ALU.add)
            tt("t0", "t0", "t2", ALU.mult)
            link(nc.vector.tensor_scalar(kg["P"], kg["t0"], sign2[:, :], None, ALU.mult))
            tt("t0", "xi", "are", ALU.mult)
            tt("t1", "xr", "aim", ALU.mult)
            tt("t0", "t0", "t1", ALU.subtract)
            tt("t0", "t0", "t2", ALU.mult)
            ts("Q", "t0", -2.0, ALU.mult)
            link(nc.vector.tensor_tensor(kg["sa"], kg["sa"], kg["mag"], ALU.mult))
            link(nc.vector.tensor_tensor(kg["sb"], kg["sb"], kg["mag"][:, :, 0:LO], ALU.mult))
            link(nc.vector.tensor_tensor(kg["U"], kg["sa"][:, :, 0:LO], kg["P"].unsqueeze(2).to_broadcast([128, D, LO]),
                                         ALU.mult))
            link(nc.vector.tensor_tensor(kg["u2"], kg["sb"], kg["Q"].unsqueeze(2).to_broadcast([128, D, LO]), ALU.mult))
            link(nc.vector.tensor_tensor(kg["U"], kg["U"], kg["u2"], ALU.add))
            assert n == KG_CHAIN, n
            def kernel_out():
                dve.wait_ge(st.kg_mm, 1)
                for q in range(4):
                    o = slice(32 * q, 32 * q + LO)
                    nc.vector.tensor_copy(kern[o, :], PS[o, 3, :]).then_inc(st.kg_dve, 1)
                dve.wait_ge(st.kg_dve, 4)
                k0 = kern[:, :].rearrange("a (d b) -> a d b", b=HI)[:, :, 0]
                for q in range(4):
                    o = slice(32 * q, 32 * q + LO)
                    nc.vector.tensor_tensor(k0[o, :], k0[o, :], dskip[o, :], ALU.add).then_inc(st.kg_dve, 1)
            steps_of(dve, dve_a, kernel_out)
            xin_a(dve, N - 1, range(GROUP))
            dve.wait_ge(st2.prep_act, 2)
            nc.vector.tensor_scalar(g_out[:, :], g_out[:, :], gates[:, 0:1], None, ALU.mult).then_inc(st2.prep_pool, 1)
            nc.vector.tensor_scalar(b_out[:, :], b_out[:, :], gates[:, 0:1], None, ALU.mult).then_inc(st2.prep_pool, 1)
            for g in range(1, N, 2):
                dve.wait_ge(st.rev, g + 1)
                nc.vector.tensor_copy(XIN[:, g * GROUP:(g + 1) * GROUP, :], PS[:, g, :].rearrange(
                    "p (j d) -> p j d", j=GROUP)).then_inc(st.rev_dve, 1)
            for q in range(1, 8, 2):
                dve.wait_ge(st.conv, q + 1)
                nc.vector.tensor_copy(Y[:, :, 16 * q:16 * q + 16], PS[:, q, :].rearrange("p (d b) -> p b d", b=B)
                                      ).then_inc(st.y_ready, 1)
            dve.wait_ge(st2.prep_pe, 1)
            nc.vector.tensor_tensor(b1p[:, :], b1[:, :], PS[:, 7, 0:CH], ALU.add).then_inc(st2.prep_pool, 1)
            nc.vector.memset(zero[:, 0:1], 0.0).then_inc(st2.prep_pool, 1)
            xt_b(dve, 0)
            steps_of(dve, dve_b)
            x1_b(dve, N - 1)
            logit_b(dve, N - 1)
            dve.wait_ge(st2.logit, N)
            gating_dve(dve)
            with dve.Fori(0, N) as i:
                relu_dve(dve, i, 0)
                for e in range(E):
                    if e + 1 < E:
                        relu_dve(dve, i, e + 1)
                    acc_dve(dve, i, e)

        @block.tensor
        def _(pe):
            pe.wait_ge(st.consts, 11)
            pe.wait_ge(st.loads_first, 16 * 15)
            tr_a(pe, 0)
            qkv_a(pe, 0)
            for h in range(H):
                scores_a(pe, 0, h)
            pe.wait_ge(st.kg_chain, KG_CHAIN)
            for d in range(D):
                q, r = d // 32, d % 32
                last = nc.tensor.matmul(PS[32 * q:32 * q + LO, 3, r * HI:(r + 1) * HI], kg["U"][:, d, :],
                                        kg["sa"][:, d, LO:NL], start=True, stop=True, skip_group_check=True)
            last.then_inc(st.kg_mm, 1)
            pe.wait_ge(st.film_params, 4)
            steps_of(pe, pe_a, lambda: pe.wait_ge(st.kg_dve, 4))
            attnT_a(pe, N - 1)
            cT_a(pe, N - 1)
            film_a(pe, N - 1)
            pe.wait_ge(st.toep_loaded, 16 * 8)
            pe.wait_ge(st.xin, N * PER["xin"])
            pe.wait_ge(st.fo, N * GROUP)
            pe.wait_ge(st.S_ready, N * H)
            for g in range(N):
                nc.tensor.matmul(PS[:, g, :], anti[:, :], XIN[:, g * GROUP:(g + 1) * GROUP, :], start=True,
                                 stop=True).then_inc(st.rev, 1)
            pe.wait_ge(st.rev_act, N // 2)
            pe.wait_ge(st.rev_dve, N // 2)
            for d in range(D):
                q, r = d // 16, d % 16
                last = nc.tensor.matmul(PS[:, q, r * B:(r + 1) * B], toep[:, d, :], XIN[:, :, d], start=True, stop=True)
                if r == 15:
                    last.then_inc(st.conv, 1)
            pe.wait_ge(st.y_ready, 8)
            pe.wait_ge(st.loads_mlp, 16 * 13)
            for c in range(CH):
                last = nc.tensor.matmul(PS[:, 7, c:c + 1], W1[:, c * 128:(c + 1) * 128], b_ffn[:, :], start=True, stop=True)
            last.then_inc(st2.prep_pe, 1)
            tr1_b(pe, 0)
            pe.wait_ge(st2.prep_pool, 4)
            pe.wait_ge(st2.prep_act, 1)
            steps_of(pe, pe_b)
            tr3_b(pe, N - 1)
            route_b(pe, N - 1)
            pe.wait_ge(st.loads_moe, 16 * (1 + E))
            pe.wait_ge(st2.x3keep, N)
            pe.wait_ge(st2.xt2, N)
            with pe.Fori(0, N) as i:
                eup_c(pe, i, 0)
                for e in range(E):
                    if e + 1 < E:
                        eup_c(pe, i, e + 1)
                    edown_c(pe, i, e)


def kernel(**inputs):
    import numpy as np
    import concourse.bacc as bacc
    from concourse.bass_utils import run_bass_kernel_spmd

    a = {k: np.asarray(v) for k, v in inputs.items()}
    p = "L0_xattn_"
    row = lambda v: v.reshape(1, -1)
    data = {
        "x": a["x"].transpose(1, 0, 2),
        "ctx": a["ctx_768"].transpose(2, 0, 1).reshape(DV, B * G),
        "text_mask": a["mask_BxS_bf1"].view(np.uint8).T,
        "ctx_mask": a["mask_BxS2_bf1"].view(np.uint8).reshape(1, B * G),
        "Wq": a[p + "Wq"], "Wk": a[p + "Wk"], "Wv": a[p + "Wv"],
        "WFi": a[p + "W_film_in"], "WFo": a[p + "W_film_out"],
        "bFi": row(a[p + "b_film_in"]), "bFo": row(a[p + "b_film_out"]),
        "g_in": row(a[p + "g_norm_in"]), "b_in": row(a[p + "b_norm_in"]), "mod": a[p + "mod_gate"].reshape(1, 1),
        "g_out": row(a[p + "g_norm_out"]), "b_out": row(a[p + "b_norm_out"]),
        "gx": a["g_xattn"].reshape(1, 1), "gf": a["g_ffn"].reshape(1, 1),
        "g_ffn": a[p + "g_ffn"].reshape(D, 1), "b_ffn": a[p + "b_ffn"].reshape(D, 1),
        "W1": a[p + "W1"], "b1": a[p + "b1"].reshape(CH, 128).T,
        "W2": a[p + "W2"].reshape(CH, 128, D).transpose(1, 0, 2), "b2": row(a[p + "b2"]),
        "ldt": row(a[p + "log_dt"]), "are": a[p + "A_re"].T, "aim": a[p + "A_im"].T, "cre": a[p + "C_re"].T,
        "cim": a[p + "C_im"].T, "dskip": row(a[p + "D_skip"]),
        "RW": a["L0_ffn_router_w"].T,
        "E1": a["L0_ffn_w1"].transpose(2, 0, 1),
        "E1b": a["L0_ffn_b1"].reshape(E, CH, 128).transpose(2, 0, 1),
        "E2": a["L0_ffn_w2"].reshape(E, D, CH, 128).transpose(3, 0, 2, 1),
        "E2b": row(a["L0_ffn_b2"]),
    }
    nc = bacc.Bacc("TRN2", target_bir_lowering=False, num_devices=1)
    arrays, t = {}, {}
    for name, v in data.items():
        v = np.ascontiguousarray(v)
        arrays[f"in_{name}"] = v
        t[name] = nc.dram_tensor(f"in_{name}", v.shape, mybir.dt.from_np(v.dtype), kind="ExternalInput").ap()
    out = nc.dram_tensor("out", (T, B, D), F32, kind="ExternalOutput").ap()
    build(nc, t, out)
    r = run_bass_kernel_spmd(nc, [arrays], core_ids=[0])
    return np.ascontiguousarray(r.results[0]["out"].transpose(1, 0, 2))
```

```python
from contextlib import ExitStack

import concourse.bass as bass
from concourse import mybir

F32 = mybir.dt.float32
F16 = mybir.dt.float16
BF16 = mybir.dt.bfloat16
I32 = mybir.dt.int32
U32 = mybir.dt.uint32
U8 = mybir.dt.uint8
ALU = mybir.AluOpType
ACT = mybir.ActivationFunctionType
AX = mybir.AxisListType

B, T, D = 32, 128, 128
G, DV = 77, 96
H, DH = 4, 32
HID = 512
CH = HID // 128
E = 8
NS = 64
GROUP = 4
N = B // GROUP
GT = GROUP * T
GG = GROUP * G
ROUNDS = 4
EPS = 1e-5
SCALE = 1.0 / float(DH) ** 0.5
MASKED = -1e30
PICKED = -3e38
LO, HI = 8, 16
NL = LO + HI
ROUND = 12582912.0
TWO_PI = 6.2831845
INV_TWO_PI = 0.15915494309189535
W_UP = 64.0
X_UP = 4.0
H_UP = 16.0


def count(i, per, k):
    return i * per + k


def wait(eng, sem, i, per, k):
    v = count(i, per, k)
    if isinstance(v, int) and v <= 0:
        return
    eng.wait_ge(sem, v)


def build(nc, t, out):
    with ExitStack() as ctx:
        def sb(name, shape, dt=F32):
            return ctx.enter_context(nc.sbuf_tensor(name, shape, dt))

        def sem(name):
            return ctx.enter_context(nc.semaphore(name))

        X = sb("X", [128, B, D])
        XL = sb("XL", [128, B, D])
        XIN = sb("XIN", [128, B, D])
        FO = sb("FO", [128, B, 2 * D])
        Y = sb("Y", [128, B, D])
        TOEP = sb("TOEP", [128, D * T])
        toep = TOEP[:, :].rearrange("s (d t) -> s d t", d=D)
        X3 = XIN[:, :, :].rearrange("p b d -> p (b d)").bitcast(F16).rearrange("p (k t) -> p k t", k=2)
        PS = ctx.enter_context(nc.psum_tensor("PS", [128, 8, 512], F32))

        Wq = sb("Wq", [D, D])
        Wk = sb("Wk", [DV, D])
        Wv = sb("Wv", [DV, D])
        WF = sb("WF", [D, 4 * D])
        film_row = sb("film_row", [33, 2, 4 * D], F16)
        part_ones = sb("part_ones", [33, T], F16)
        ones_bf = sb("ones_bf", [128, T], BF16)
        row_params = sb("row_params", [128, 4 * D + 3])
        g_in, b_in, g_out, b_out = (row_params[:, k * D:(k + 1) * D] for k in range(4))
        mod = row_params[:, 4 * D:4 * D + 1]
        gates = row_params[:, 4 * D + 1:4 * D + 3]
        text_mask = sb("text_mask", [128, B], U8)
        text_w = sb("text_w", [128, B])
        ctx_mask = sb("ctx_mask", [128, B * G], U8)
        W1 = sb("W1", [D, HID])
        W2 = sb("W2", [128, CH, D])
        b1 = sb("b1", [128, CH])
        b2row = sb("b2row", [1, D])
        g_ffn = sb("g_ffn", [D, 1])
        b_ffn = sb("b_ffn", [D, 1])
        RW = sb("RW", [D, E])
        E1b = sb("E1b", [128, E, CH])
        E2b = sb("E2b", [33, E, D])
        film_bias = E2b[:, 0:4, :].rearrange("p e d -> p (e d)")
        ident = sb("ident", [128, 128])
        anti = sb("anti", [128, 128])
        ones = sb("ones", [128, 128])
        mhalf = sb("mhalf", [128, GROUP])
        eps = sb("eps", [128, GROUP])
        idle = sb("idle", [1, 1])

        taken = 0

        def scratch(width):
            nonlocal taken
            taken += width
            assert taken <= B * D
            return Y[:, :, :].rearrange("p b d -> p (b d)")[:, taken - width:taken]

        ctx_T = sb("ctx_T", [DV, GG])
        stats = sb("stats", [128, GROUP, 6])
        mv = sb("mv", [128, GROUP, 2])
        rs = sb("rs", [128, 8, GROUP])
        xl = sb("xl", [128, GROUP, D])
        xlT = sb("xlT", [128, GT])
        QT = sb("QT", [128, GT])
        KT = sb("KT", [128, GG])
        V = sb("V", [G, GROUP, D])
        V_next = sb("V_next", [G, GROUP, D])
        bias_rows = sb("bias_rows", [128, GG], BF16)
        S = scratch(H * GROUP * G).rearrange("p (h j g) -> p h j g", h=H, j=GROUP)
        left = scratch(GROUP * G).rearrange("p (j g) -> p j g", j=GROUP)
        top = sb("top", [128, ROUNDS, GROUP, 8])
        neg_max = sb("neg_max", [128, H, GROUP])
        P = scratch(H * GROUP * G).rearrange("p (h j g) -> p h j g", h=H, j=GROUP)
        A = scratch(H * GROUP * G).rearrange("p (h j g) -> p h j g", h=H, j=GROUP)
        total = sb("total", [128, H, GROUP])
        share = sb("share", [128, H, GROUP])
        AT = sb("AT", [G, GT])
        CT = sb("CT", [128, GT])
        tmp = sb("tmp", [128, GROUP, D])

        kg = {}
        at = 0
        for name in ("are", "aim", "cre", "cim", "ldt", "dt", "re", "tu", "th", "s2", "c2", "t0", "t1", "t2",
                     "em", "q", "nr", "ni", "xr", "xi", "P", "Q"):
            kg[name] = TOEP[:, at:at + D]
            at += D
        for name, w in (("mag", NL), ("sa", NL), ("ta", NL), ("tb", LO), ("sb", LO), ("U", LO), ("u2", LO)):
            kg[name] = TOEP[:, at:at + D * w].rearrange("p (d l) -> p d l", l=w)
            at += D * w
        assert at <= D * T
        steps_i = sb("steps_i", [128, NL], I32)
        steps = sb("steps", [128, NL])
        quarter = sb("quarter", [128, 2])
        sign2 = sb("sign2", [128, 1])
        minus1 = sb("minus1", [128, D])
        kern = sb("kern", [128, 32 * HI])
        dskip = sb("dskip", [128, 32])
        zero = sb("zero", [128, 128])
        kpad = nc.dram_tensor("kpad", [D, 2 * T], F32, kind="Internal")

        S_ = {}
        for name in """loads_first loads_kernel loads_skip kg_mag loads_mlp loads_moe x_loaded ctx_loaded bn_done consts kg_chain kg_dve kg_act
            kg_mm kpad_written toep_loaded masks masks_clear v_moved rev rev_act rev_dve film_params stats_a rstd_a norm_a pool_a tr_a trev_a bias_ready qkv
            qkvev scores S_ready max_done repl_done neg_done exp_done sel_done sum_done share_done weights attnT
            attnTev cT cTev film fo xin conv y_ready""".split():
            S_[name] = sem(name)

        st = type("Sems", (), S_)

        def sl(i):
            return bass.ds(i * GROUP, GROUP)

        def apart(eng, i):
            if not isinstance(i, int):
                nc.vector.memset(idle[:, :], 0.0)

        PER = dict(stats=GROUP, rstd=8, norm=GROUP, pool=7, tr=1, trev=1, bias=1, qkv=3, qkvev=3, scores=H,
                   S=H, neg=H, exp=H * GROUP, sel=H, sum=H,
                   share=2, weights=1, attnT=1, attnTev=1, cT=1, cTev=1, film=GROUP, fo=GROUP, xin=2 * GROUP)

        def mean_var(eng, src, mvt, signal):
            for j in range(GROUP):
                nc.vector.bn_stats(stats[:, j, :], src(j)).then_inc(st.bn_done, 1)
            for j in range(GROUP):
                eng.wait_ge(st.bn_done, j + 1)
                nc.vector.bn_aggr(mvt[:, j, :], stats[:, j, :]).then_inc(signal, 1)
            eng.sem_clear(st.bn_done)

        def stats_a(eng, i):
            wait(eng, st.x_loaded, i, 16, 16)
            wait(eng, st.norm_a, i, GROUP, 0)
            wait(eng, st.rstd_a, i, 8, 0)
            apart(eng, i)
            mean_var(eng, lambda j: X[:, bass.ds(i * GROUP + j, 1), :], mv, st.stats_a)

        def rstd_a(eng, i):
            wait(eng, st.stats_a, i, PER["stats"], GROUP)
            wait(eng, st.norm_a, i, GROUP, 0)
            wait(eng, st.pool_a, i, PER["pool"], 0)
            mean, var = mv[:, :, 0], mv[:, :, 1]
            ve, r, nmr, vr, r2 = (rs[:, k, :] for k in range(5))
            k = 0

            def step(ins):
                nonlocal k
                k += 1
                ins.then_inc(st.rstd_a, 1)

            def last():
                wait(eng, st.rstd_a, i, 8, k)

            step(nc.gpsimd.tensor_tensor(ve, var, eps[:, :], ALU.add))
            last()
            step(nc.gpsimd.tensor_tensor(r, ve, mhalf[:, :], ALU.pow))
            last()
            step(nc.gpsimd.tensor_tensor(nmr, mean, r, ALU.mult))
            last()
            step(nc.gpsimd.tensor_tensor(nmr, nmr, minus1[:, 0:GROUP], ALU.mult))
            step(nc.gpsimd.tensor_tensor(vr, var, r, ALU.mult))
            last()
            step(nc.gpsimd.tensor_tensor(vr, vr, r, ALU.mult))
            last()
            step(nc.gpsimd.tensor_tensor(vr, vr, eps[:, :], ALU.add))
            last()
            step(nc.gpsimd.tensor_tensor(r2, vr, mhalf[:, :], ALU.pow))

        def norm_a(eng, i):
            wait(eng, st.rstd_a, i, 8, 4)
            wait(eng, st.pool_a, i, PER["pool"], 0)
            wait(eng, st.tr_a, i, 1, 0)
            for j in range(GROUP):
                nc.scalar.activation(xl[:, j, :], X[:, bass.ds(i * GROUP + j, 1), :], ACT.Identity,
                                     bias=rs[:, 2, j:j + 1], scale=rs[:, 1, j:j + 1]).then_inc(st.norm_a, 1)

        def affine_a(eng, i):
            wait(eng, st.norm_a, i, GROUP, GROUP)
            wait(eng, st.rstd_a, i, 8, 8)
            nc.gpsimd.tensor_copy(XL[:, sl(i), :], xl[:, :, :]).then_inc(st.pool_a, 1)
            for j in range(GROUP):
                nc.gpsimd.tensor_scalar(tmp[:, j, :], xl[:, j, :], rs[:, 4, j:j + 1], None,
                                        ALU.mult).then_inc(st.pool_a, 1)
            wait(eng, st.pool_a, i, PER["pool"], 1 + GROUP)
            nc.gpsimd.tensor_tensor(tmp[:, :, :], tmp[:, :, :], g_in[:, :].unsqueeze(1).to_broadcast([128, GROUP, D]),
                                    ALU.mult).then_inc(st.pool_a, 1)
            wait(eng, st.pool_a, i, PER["pool"], 2 + GROUP)
            nc.gpsimd.tensor_tensor(XIN[:, sl(i), :], tmp[:, :, :],
                                    b_in[:, :].unsqueeze(1).to_broadcast([128, GROUP, D]),
                                    ALU.add).then_inc(st.pool_a, 1)

        def bias_a(eng, i):
            wait(eng, st.scores, i, H, 0)
            nc.vector.tensor_scalar(bias_rows[0:97, :], ctx_mask[0:97, bass.ds(i * GG, GG)], -MASKED, MASKED,
                                    ALU.mult, ALU.add).then_inc(st.bias_ready, 1)

        def tr_a(eng, i):
            wait(eng, st.norm_a, i, GROUP, GROUP)
            wait(eng, st.fo, i - 2, GROUP, 0)
            wait(eng, st.xin, i - 2, PER["xin"], 0)
            wait(eng, st.qkvev, i, 3, 0)
            for j in range(GROUP):
                last = nc.tensor.transpose(PS[:, 0, j * T:(j + 1) * T], xl[:, j, :], ident[:, :])
            last.then_inc(st.tr_a, 1)

        def trev_a(eng, i):
            wait(eng, st.tr_a, i, 1, 1)
            wait(eng, st.qkv, i, 3, 0)
            nc.scalar.activation(xlT[:, :], PS[:, 0, :], ACT.Copy).then_inc(st.trev_a, 1)

        def qkv_a(eng, i):
            wait(eng, st.trev_a, i, 1, 1)
            wait(eng, st.ctx_loaded, i, 16, 16)
            nc.tensor.matmul(PS[:, 1, :], Wq[:, :], xlT[:, :], start=True, stop=True).then_inc(st.qkv, 1)
            nc.tensor.matmul(PS[:, 2, 0:GG], Wk[:, :], ctx_T[:, :], start=True, stop=True).then_inc(st.qkv, 1)
            for j in range(GROUP):
                last = nc.tensor.matmul(PS[0:G, 0, j * D:(j + 1) * D], ctx_T[:, j * G:(j + 1) * G], Wv[:, :],
                                        start=True, stop=True)
            last.then_inc(st.qkv, 1)

        def qkvev_a(eng, i):
            wait(eng, st.scores, i, H, 0)
            wait(eng, st.qkv, i, 3, 1)
            nc.scalar.activation(QT[:, :], PS[:, 1, :], ACT.Copy).then_inc(st.qkvev, 1)
            wait(eng, st.qkv, i, 3, 2)
            nc.scalar.activation(KT[:, :], PS[:, 2, 0:GG], ACT.Copy).then_inc(st.qkvev, 1)

        def vev_a(eng, i):
            wait(eng, st.qkv, i, 3, 3)
            wait(eng, st.v_moved, i, 1, 0)
            nc.scalar.activation(V_next[:, :, :].rearrange("g j d -> g (j d)"), PS[0:G, 0, :],
                                 ACT.Copy).then_inc(st.qkvev, 1)

        def v_a(eng, i):
            wait(eng, st.cT, i, 1, 0)
            wait(eng, st.qkvev, i, 3, 3)
            nc.gpsimd.tensor_tensor(V[:, :, :], V_next[:, :, :],
                                    ones[0:G, :].unsqueeze(1).to_broadcast([G, GROUP, D]), ALU.mult).then_inc(st.v_moved, 1)

        def scores_a(eng, i, h):
            if h == 0:
                wait(eng, st.qkvev, i, 3, 2)
                wait(eng, st.bias_ready, i, 1, 1)
            wait(eng, st.S_ready, i, H, h + 1 - H)
            r = slice(h * DH, (h + 1) * DH)
            o = slice(h * DH, h * DH + 1)
            nc.tensor.matmul(PS[:, 4 + h, 0:GG], ones_bf[o, :], bias_rows[o, :], start=True, stop=False)
            for j in range(GROUP):
                last = nc.tensor.matmul(PS[:, 4 + h, j * G:(j + 1) * G], QT[r, j * T:(j + 1) * T],
                                        KT[r, j * G:(j + 1) * G], start=False, stop=j == GROUP - 1)
            last.then_inc(st.scores, 1)

        def s_a(eng, i, h):
            wait(eng, st.scores, i, H, h + 1)
            wait(eng, st.sel_done, i, H, h + 1 - H)
            wait(eng, st.exp_done, i, PER["exp"], (h + 1) * GROUP - PER["exp"])
            nc.scalar.activation(S[:, h, :, :].rearrange("p j g -> p (j g)"), PS[:, 4 + h, 0:GG], ACT.Copy,
                                 scale=SCALE).then_inc(st.S_ready, 1)

        def topk_a(eng, i, h):
            wait(eng, st.S_ready, i, H, h + 1)
            apart(eng, i)
            for r in range(ROUNDS):
                for j in range(GROUP):
                    if r:
                        eng.wait_ge(st.repl_done, (r - 1) * GROUP + j + 1)
                    src = left[:, j, :] if r else S[:, h, j, :]
                    nc.vector.max(top[:, r, j, :], src).then_inc(st.max_done, 1)
                for j in range(GROUP):
                    eng.wait_ge(st.max_done, r * GROUP + j + 1)
                    src = left[:, j, :] if r else S[:, h, j, :]
                    nc.vector.match_replace(left[:, j, :], top[:, r, j, :], src, PICKED).then_inc(st.repl_done, 1)
                if r == 0:
                    wait(eng, st.exp_done, i, PER["exp"], (h + 1) * GROUP - PER["exp"])
                    nc.vector.tensor_scalar(neg_max[:, h, :], top[:, 0, :, 0], -1.0, None,
                                            ALU.mult).then_inc(st.neg_done, 1)
            wait(eng, st.exp_done, i, PER["exp"], (h + 1) * GROUP)
            eng.wait_ge(st.repl_done, ROUNDS * GROUP)
            p, l = P[:, h, :, :], left[:, :, :]
            nc.vector.scalar_tensor_tensor(out=p, in0=l, scalar=PICKED, in1=p, op0=ALU.is_equal,
                                           op1=ALU.mult).then_inc(st.sel_done, 1)
            wait(eng, st.sel_done, i, H, h + 1)
            nc.vector.tensor_reduce(total[:, h, :], p, AX.X, ALU.add).then_inc(st.sum_done, 1)
            eng.sem_clear(st.max_done)
            eng.sem_clear(st.repl_done)

        def exp_a(eng, i, h):
            wait(eng, st.neg_done, i, H, h + 1)
            wait(eng, st.weights, i, 1, 0)
            for j in range(GROUP):
                nc.scalar.activation(P[:, h, j, :], S[:, h, j, :], ACT.Exp,
                                     bias=neg_max[:, h, j:j + 1]).then_inc(st.exp_done, 1)

        def share_a(eng, i):
            wait(eng, st.sum_done, i, H, H)
            wait(eng, st.weights, i, 1, 0)
            nc.vector.reciprocal(share[:, :, :], total[:, :, :]).then_inc(st.share_done, 1)
            wait(eng, st.share_done, i, 2, 1)
            nc.vector.tensor_tensor(share[:, :, :], share[:, :, :],
                                    text_w[:, sl(i)].unsqueeze(1).to_broadcast([128, H, GROUP]),
                                    ALU.mult).then_inc(st.share_done, 1)

        def weights_a(eng, i):
            wait(eng, st.share_done, i, 2, 2)
            wait(eng, st.attnT, i, 1, 0)
            nc.gpsimd.tensor_tensor(A[:, :, :, :].rearrange("p h j g -> p (h j) g"),
                                    P[:, :, :, :].rearrange("p h j g -> p (h j) g"),
                                    share[:, :, :].rearrange("p h j -> p (h j)").unsqueeze(2)
                                    .to_broadcast([128, H * GROUP, G]), ALU.mult).then_inc(st.weights, 1)

        def attnT_a(eng, i):
            wait(eng, st.weights, i, 1, 1)
            wait(eng, st.fo, i, GROUP, 0)
            wait(eng, st.xin, i, PER["xin"], 0)
            for j in range(GROUP):
                for h in range(H):
                    last = nc.tensor.matmul(PS[0:G, 3, j * T:(j + 1) * T], A[:, h, j, :], ident[:, :],
                                            start=h == 0, stop=h == H - 1)
            last.then_inc(st.attnT, 1)

        def attnTev_a(eng, i):
            wait(eng, st.attnT, i, 1, 1)
            wait(eng, st.cT, i, 1, 0)
            nc.scalar.activation(AT[:, :], PS[0:G, 3, :], ACT.Copy).then_inc(st.attnTev, 1)

        def cT_a(eng, i):
            wait(eng, st.attnTev, i, 1, 1)
            wait(eng, st.v_moved, i, 1, 1)
            for j in range(GROUP):
                last = nc.tensor.matmul(PS[:, 3, j * T:(j + 1) * T], V[:, j, :], AT[:, j * T:(j + 1) * T],
                                        start=True, stop=True)
            last.then_inc(st.cT, 1)

        def cTev_a(eng, i):
            wait(eng, st.cT, i, 1, 1)
            wait(eng, st.film, i, GROUP, 0)
            nc.scalar.activation(CT[:, :], PS[:, 3, :], ACT.Copy).then_inc(st.cTev, 1)

        bank_of = (1, 2, 0, 3)

        def film_a(eng, i):
            wait(eng, st.cTev, i, 1, 1)
            last = min(i + 2, N - 1) if isinstance(i, int) else i + 2
            wait(eng, st.qkvev, last, 3, 3)
            for j in range(GROUP):
                nc.tensor.matmul(PS[:, bank_of[j], :], part_ones[:, :], film_row[:, 0, :], start=True, stop=False)
                nc.tensor.matmul(PS[:, bank_of[j], :], CT[:, j * T:(j + 1) * T], WF[:, :], start=False,
                                 stop=True).then_inc(st.film, 1)

        def fo_a(eng, i, js):
            for j in js:
                wait(eng, st.film, i, GROUP, j + 1)
                nc.scalar.activation(FO[:, bass.ds(i * GROUP + j, 1), :], PS[:, bank_of[j], 2 * D:],
                                     ACT.Copy).then_inc(st.fo, 1)

        def xin_a(eng, i, js):
            wait(eng, st.pool_a, i, PER["pool"], 3 + GROUP)
            for j in js:
                wait(eng, st.fo, i, GROUP, j + 1)
                z = XIN[:, bass.ds(i * GROUP + j, 1), :]
                nc.vector.tensor_tensor(z, z, PS[:, bank_of[j], 0:D].unsqueeze(1), ALU.mult).then_inc(st.xin, 1)
                wait(eng, st.xin, i, PER["xin"], 2 * j + 1)
                nc.vector.tensor_tensor(z, z, PS[:, bank_of[j], D:2 * D].unsqueeze(1), ALU.add).then_inc(st.xin, 1)

        def dve_a(eng, i, has_prev, has_next):
            if has_next:
                stats_a(eng, i + 1)
                bias_a(eng, i + 1)
            topk_a(eng, i, 0)
            topk_a(eng, i, 1)
            topk_a(eng, i, 2)
            if has_prev:
                xin_a(eng, i - 1, (0, 1))
            topk_a(eng, i, 3)
            share_a(eng, i)
            if has_prev:
                xin_a(eng, i - 1, (2, 3))

        def pool_a(eng, i, has_prev, has_next):
            if has_next:
                rstd_a(eng, i + 1)
                affine_a(eng, i + 1)
            v_a(eng, i)
            weights_a(eng, i)

        def act_a(eng, i, has_prev, has_next):
            if has_next:
                norm_a(eng, i + 1)
            exp_a(eng, i, 0)
            s_a(eng, i, 3)
            if has_prev:
                attnTev_a(eng, i - 1)
            if has_next:
                trev_a(eng, i + 1)
            exp_a(eng, i, 1)
            if has_prev:
                cTev_a(eng, i - 1)
            if has_next:
                qkvev_a(eng, i + 1)
                vev_a(eng, i + 1)
                s_a(eng, i + 1, 0)
            exp_a(eng, i, 2)
            if has_next:
                s_a(eng, i + 1, 1)
            if has_prev:
                fo_a(eng, i - 1, (0, 1))
            exp_a(eng, i, 3)
            if has_prev:
                fo_a(eng, i - 1, (2, 3))
            if has_next:
                s_a(eng, i + 1, 2)

        def pe_a(eng, i, has_prev, has_next):
            if has_prev:
                attnT_a(eng, i - 1)
            if has_next:
                tr_a(eng, i + 1)
            if has_prev:
                cT_a(eng, i - 1)
            if has_next:
                qkv_a(eng, i + 1)
                scores_a(eng, i + 1, 0)
                scores_a(eng, i + 1, 1)
            if has_prev:
                film_a(eng, i - 1)
            if has_next:
                scores_a(eng, i + 1, 2)
                scores_a(eng, i + 1, 3)

        def steps_of(eng, body, between=()):
            for i in range(2):
                body(eng, i, i > 0, True)
                if i < len(between):
                    between[i]()
            with eng.Fori(2, N - 1) as i:
                body(eng, i, True, True)
            body(eng, N - 1, True, False)

        late_at = 3 * E * HID

        def late(width):
            nonlocal late_at
            late_at += width
            assert late_at <= D * T
            return TOEP[:, late_at - width:late_at]

        hs, hT, x2n, x3T = tmp, xlT, xl, QT
        x3 = late(GROUP * D).rearrange("p (j d) -> p j d", j=GROUP)
        hid = late(CH * GT).rearrange("p (c t) -> p c t", c=CH)
        b1p = sb("b1p", [128, CH])
        W1g = sb("W1g", [D, HID])
        mv1, mv2, mv3 = sb("mv1", [128, GROUP, 2]), sb("mv2", [128, GROUP, 2]), sb("mv3", [128, GROUP, 2])
        rs1, rs2, rs3 = sb("rs1", [128, 3, GROUP]), sb("rs2", [128, 3, GROUP]), sb("rs3", [128, 3, GROUP])
        logits = late(B * E).rearrange("p (b e) -> p b e", e=E)
        for name in """prep_pe prep_act prep_pool xt s1 r1 n1 tr1 tr1ev up act down xt2 s2 r2 n2 xb x1 s3 r3 n3 tr3 tr3ev x3high x3keep
            route logit""".split():
            S_[name] = sem(name)
        st2 = type("Sems2", (), S_)

        def norm_stats(eng, i, src, mvt, signal):
            apart(eng, i)
            mean_var(eng, src, mvt, signal)

        def norm_factors(eng, i, mvt, rst, have, signal, used):
            wait(eng, have, i, GROUP, GROUP)
            wait(eng, used, i, GROUP, 0)
            nc.gpsimd.tensor_tensor(rst[:, 0, :], mvt[:, :, 1], eps[:, :], ALU.add).then_inc(signal, 1)
            wait(eng, signal, i, 4, 1)
            nc.gpsimd.tensor_tensor(rst[:, 1, :], rst[:, 0, :], mhalf[:, :], ALU.pow).then_inc(signal, 1)
            wait(eng, signal, i, 4, 2)
            nc.gpsimd.tensor_tensor(rst[:, 2, :], mvt[:, :, 0], rst[:, 1, :], ALU.mult).then_inc(signal, 1)
            wait(eng, signal, i, 4, 3)
            nc.gpsimd.tensor_tensor(rst[:, 2, :], rst[:, 2, :], minus1[:, 0:GROUP], ALU.mult).then_inc(signal, 1)

        def normalise(eng, i, dst, src, rst, have, signal):
            wait(eng, have, i, 4, 4)
            for j in range(GROUP):
                nc.scalar.activation(dst(j), src(j), ACT.Identity, bias=rst[:, 2, j:j + 1],
                                     scale=rst[:, 1, j:j + 1]).then_inc(signal, 1)

        def row(arr, i, j):
            return arr[:, bass.ds(i * GROUP + j, 1), :]

        def xt_b(eng, i):
            y = Y[:, sl(i), :]
            if isinstance(i, int) and i == 0:
                eng.wait_ge(st.y_ready, 8)
            nc.vector.tensor_tensor(y, y, FO[:, sl(i), 0:D], ALU.mult).then_inc(st2.xt, 1)
            wait(eng, st2.xt, i, 3, 1)
            nc.vector.tensor_tensor(y, y, FO[:, sl(i), D:2 * D], ALU.add).then_inc(st2.xt, 1)
            wait(eng, st2.xt, i, 3, 2)
            nc.vector.tensor_tensor(y, y, XL[:, sl(i), :], ALU.add).then_inc(st2.xt, 1)
            wait(eng, st2.xt, i, 3, 3)
            wait(eng, st2.r1, i, 4, 0)
            norm_stats(eng, i, lambda j: row(Y, i, j), mv1, st2.s1)

        def n1_b(eng, i):
            wait(eng, st2.tr1, i, 1, 0)
            normalise(eng, i, lambda j: hs[:, j, :], lambda j: row(Y, i, j), rs1, st2.r1, st2.n1)

        def tr1_b(eng, i):
            wait(eng, st2.n1, i, GROUP, GROUP)
            wait(eng, st2.tr1ev, i, 1, 0)
            for j in range(GROUP):
                last = nc.tensor.transpose(PS[:, 0, j * T:(j + 1) * T], hs[:, j, :], ident[:, :])
            last.then_inc(st2.tr1, 1)

        def tr1ev_b(eng, i):
            wait(eng, st2.tr1, i, 1, 1)
            wait(eng, st2.up, i, CH, 0)
            nc.scalar.activation(hT[:, :], PS[:, 0, :], ACT.Copy).then_inc(st2.tr1ev, 1)

        def up_b(eng, i):
            wait(eng, st2.tr1ev, i, 1, 1)
            for c in range(CH):
                wait(eng, st2.act, i, CH, c + 1 - CH)
                nc.tensor.matmul(PS[:, 1 + c, :], W1g[:, c * 128:(c + 1) * 128], hT[:, :], start=True,
                                 stop=True).then_inc(st2.up, 1)

        def gelu_b(eng, i):
            wait(eng, st2.down, i, 1, 0)
            for c in range(CH):
                wait(eng, st2.up, i, CH, c + 1)
                nc.scalar.activation(hid[:, c, :], PS[:, 1 + c, :], ACT.Gelu, bias=b1p[:, c:c + 1]).then_inc(st2.act, 1)

        def down_b(eng, i):
            wait(eng, st2.act, i, CH, CH)
            wait(eng, st2.xt2, i, 1, 0)
            for j in range(GROUP):
                o = PS[:, 5, j * D:(j + 1) * D]
                nc.tensor.matmul(o, ones[0:1, :], b2row[:, :], start=True, stop=False)
                for c in range(CH):
                    last = nc.tensor.matmul(o, hid[:, c, j * T:(j + 1) * T], W2[:, c, :], start=False, stop=c == CH - 1)
            last.then_inc(st2.down, 1)

        def xt2_b(eng, i):
            wait(eng, st2.down, i, 1, 1)
            wait(eng, st2.n1, i, GROUP, GROUP)
            y = Y[:, sl(i), :]
            nc.vector.tensor_tensor(y, y, PS[:, 5, :].rearrange("p (j d) -> p j d", j=GROUP),
                                    ALU.add).then_inc(st2.xt2, 1)
            wait(eng, st2.xt2, i, 1, 1)
            wait(eng, st2.r2, i, 4, 0)
            norm_stats(eng, i, lambda j: row(Y, i, j), mv2, st2.s2)

        def n2_b(eng, i):
            wait(eng, st2.x1, i, 2, 0)
            normalise(eng, i, lambda j: x2n[:, j, :], lambda j: row(Y, i, j), rs2, st2.r2, st2.n2)

        def xb_b(eng, i):
            nc.gpsimd.tensor_tensor(X[:, sl(i), :], X[:, sl(i), :],
                                    b_out[:, :].unsqueeze(1).to_broadcast([128, GROUP, D]), ALU.add).then_inc(st2.xb, 1)

        def x1_b(eng, i):
            wait(eng, st2.n2, i, GROUP, GROUP)
            wait(eng, st2.xb, i, 1, 1)
            nc.vector.tensor_tensor(x2n[:, :, :], x2n[:, :, :], g_out[:, :].unsqueeze(1).to_broadcast([128, GROUP, D]),
                                    ALU.mult).then_inc(st2.x1, 1)
            wait(eng, st2.x1, i, 2, 1)
            nc.vector.tensor_tensor(X[:, sl(i), :], X[:, sl(i), :], x2n[:, :, :], ALU.add).then_inc(st2.x1, 1)
            wait(eng, st2.x1, i, 2, 2)
            wait(eng, st2.r3, i, 4, 0)
            norm_stats(eng, i, lambda j: row(X, i, j), mv3, st2.s3)

        def n3_b(eng, i):
            wait(eng, st2.tr3, i, 1, 0)
            normalise(eng, i, lambda j: x3[:, j, :], lambda j: row(X, i, j), rs3, st2.r3, st2.n3)

        def tr3_b(eng, i):
            wait(eng, st2.n3, i, GROUP, GROUP)
            wait(eng, st2.x3high, i, 1, 0)
            for j in range(GROUP):
                last = nc.tensor.transpose(PS[:, 6, j * T:(j + 1) * T], x3[:, j, :], ident[:, :])
            last.then_inc(st2.tr3, 1)

        def tr3ev_b(eng, i):
            wait(eng, st2.tr3, i, 1, 1)
            wait(eng, st2.x3keep, i, 1, 0)
            wait(eng, st2.route, i, 1, 0)
            nc.scalar.activation(x3T[:, :], PS[:, 6, :], ACT.Copy).then_inc(st2.tr3ev, 1)
            nc.scalar.activation(X3[:, 0, bass.ds(i * GT, GT)], PS[:, 6, :], ACT.Copy, scale=X_UP).then_inc(st2.x3high, 1)

        def keep_b(eng, i):
            wait(eng, st2.tr3ev, i, 1, 1)
            wait(eng, st2.x3high, i, 1, 1)
            nc.vector.scalar_tensor_tensor(out=X3[:, 1, bass.ds(i * GT, GT)], in0=x3T[:, :], scalar=X_UP,
                                           in1=X3[:, 0, bass.ds(i * GT, GT)], op0=ALU.mult,
                                           op1=ALU.subtract).then_inc(st2.x3keep, 1)

        def route_b(eng, i):
            wait(eng, st2.tr3ev, i, 1, 1)
            wait(eng, st2.logit, i, 1, 0)
            for j in range(GROUP):
                last = nc.tensor.matmul(PS[:, 7, j * E:(j + 1) * E], x3T[:, j * T:(j + 1) * T], RW[:, :], start=True,
                                        stop=True)
            last.then_inc(st2.route, 1)

        def logit_b(eng, i):
            wait(eng, st2.route, i, 1, 1)
            nc.vector.tensor_copy(logits[:, sl(i), :], PS[:, 7, 0:GROUP * E].rearrange("p (j e) -> p j e", e=E)
                                  ).then_inc(st2.logit, 1)

        def dve_b(eng, i, has_prev, has_next):
            if has_next:
                xt_b(eng, i + 1)
            if has_prev:
                x1_b(eng, i - 1)
            xt2_b(eng, i)
            if has_prev:
                logit_b(eng, i - 1)
                keep_b(eng, i - 1)

        def pool_b(eng, i, has_prev, has_next):
            if has_next:
                norm_factors(eng, i + 1, mv1, rs1, st2.s1, st2.r1, st2.n1)
            if has_prev:
                norm_factors(eng, i - 1, mv3, rs3, st2.s3, st2.r3, st2.n3)
            xb_b(eng, i)
            norm_factors(eng, i, mv2, rs2, st2.s2, st2.r2, st2.n2)

        def act_b(eng, i, has_prev, has_next):
            if has_prev:
                n2_b(eng, i - 1)
            gelu_b(eng, i)
            if has_next:
                n1_b(eng, i + 1)
            if has_prev:
                n3_b(eng, i - 1)
            if has_next:
                tr1ev_b(eng, i + 1)
            if has_prev:
                tr3ev_b(eng, i - 1)

        def pe_b(eng, i, has_prev, has_next):
            up_b(eng, i)
            down_b(eng, i)
            if has_next:
                tr1_b(eng, i + 1)
            if has_prev:
                tr3_b(eng, i - 1)
                route_b(eng, i - 1)

        def room(which, pattern, dt=F32, **dims):
            return TOEP[:, which * E * HID:(which + 1) * E * HID].bitcast(dt).rearrange(pattern, **dims)

        E1, E2 = room(0, "p (e f) -> p e f", e=E), room(1, "p (e f) -> p e f", e=E)
        E1s = room(2, "p (k e f) -> p k e f", F16, k=2, e=E)
        E2s = room(0, "p (k e c d) -> p k e c d", F16, k=2, e=E, c=CH)
        E2s_flat = room(0, "p (k e f) -> p k e f", F16, k=2, e=E)
        hid32 = room(1, "p (s c t) -> p s c t", s=2, c=CH)
        hids = XL[:, :, :].rearrange("p b d -> p (b d)").bitcast(F16).rearrange("p (s k c t) -> p s k c t", s=2, k=2, c=CH)
        b2s = V_next[0:33, :, :].rearrange("p j d -> p (j d)").bitcast(F16).rearrange("p (e d) -> p e d", e=E)
        b2_high = V[32:33, :, :].rearrange("p j d -> p (j d)").bitcast(F16).rearrange("p (e d) -> p e d", e=E)
        b2_ones = KT[0:33, 0:T // 2].bitcast(F16)
        gate = late(B * E).rearrange("p (b e) -> p b e", e=E)
        gw = sb("gw", [128, 6, B])
        gx = late(2 * B * E).rearrange("p (k b e) -> p k b e", k=2, e=E)
        m8 = late(B * 8).rearrange("p (b e) -> p b e", e=8)
        i8 = late(B * 8).bitcast(U32).rearrange("p (b e) -> p b e", e=8)
        i8f = sb("i8f", [128, B, 2])
        eid_i = sb("eid_i", [128, E], I32)
        eid = sb("eid", [128, E])
        for name in "gate_dve gate_act eup relu high low split_high split_low bias_prep edown eacc stored".split():
            S_[name] = sem(name)
        st3 = type("Sems3", (), S_)

        def gating_dve(eng):
            n = 0

            def link(ins):
                nonlocal n
                n += 1
                ins.then_inc(st3.gate_dve, 1)
                eng.wait_ge(st3.gate_dve, n)

            for b in range(B):
                nc.vector.max(m8[:, b, :], logits[:, b, :]).then_inc(st3.gate_dve, 1)
            eng.wait_ge(st3.gate_dve, B)
            for b in range(B):
                nc.vector.max_index(i8[:, b, :], m8[:, b, :], logits[:, b, :]).then_inc(st3.gate_dve, 1)
            n = 2 * B
            eng.wait_ge(st3.gate_dve, n)
            link(nc.vector.tensor_copy(i8f[:, :, :], i8[:, :, 0:2]))
            link(nc.vector.tensor_tensor(gx[:, 0, :, :], logits[:, :, :], m8[:, :, 0:1].to_broadcast([128, B, E]),
                                         ALU.subtract))
            link(nc.vector.tensor_tensor(gw[:, 0, :], m8[:, :, 1], m8[:, :, 0], ALU.subtract))
            eng.wait_ge(st3.gate_act, 2)
            link(nc.vector.tensor_reduce(gw[:, 2, :], gx[:, 1, :, :], AX.X, ALU.add))
            link(nc.vector.scalar_tensor_tensor(out=gw[:, 3, :], in0=gw[:, 2, :], scalar=1e-9, in1=gw[:, 1, :],
                                                op0=ALU.mult, op1=ALU.add))
            link(nc.vector.tensor_scalar(gw[:, 3, :], gw[:, 3, :], 1.0, None, ALU.add))
            link(nc.vector.reciprocal(gw[:, 4, :], gw[:, 3, :]))
            link(nc.vector.tensor_scalar(gw[:, 4, :], gw[:, 4, :], gates[:, 1:2], 1.0 / (W_UP * H_UP), ALU.mult, ALU.mult))
            link(nc.vector.tensor_tensor(gw[:, 5, :], gw[:, 4, :], gw[:, 1, :], ALU.mult))
            ids = eid[:, :].unsqueeze(1).to_broadcast([128, B, E])
            for k in range(2):
                link(nc.vector.tensor_tensor(gx[:, k, :, :], ids, i8f[:, :, k:k + 1].to_broadcast([128, B, E]),
                                             ALU.is_equal))
                link(nc.vector.tensor_tensor(gx[:, k, :, :], gx[:, k, :, :],
                                             gw[:, 4 + k, :].unsqueeze(2).to_broadcast([128, B, E]), ALU.mult))
            link(nc.vector.tensor_tensor(gate[:, :, :], gx[:, 0, :, :], gx[:, 1, :, :], ALU.add))

        def gating_act(eng):
            eng.wait_ge(st3.gate_dve, 2 * B + 3)
            nc.scalar.activation(gx[:, 1, :, :], gx[:, 0, :, :], ACT.Exp).then_inc(st3.gate_act, 1)
            nc.scalar.activation(gw[:, 1, :], gw[:, 0, :], ACT.Exp).then_inc(st3.gate_act, 1)

        def eup_c(eng, i, e):
            for c in range(CH):
                wait(eng, st3.relu, i, CH * E, CH * (e - 1) + c + 1)
                w = [E1s[:, k, e, c * 128:(c + 1) * 128] for k in range(2)]
                x = [X3[:, k, bass.ds(i * GT, GT)] for k in range(2)]
                nc.tensor.matmul(PS[:, c, :], w[0], x[0], start=True, stop=False)
                nc.tensor.matmul(PS[:, c, :], w[0], x[1], start=False, stop=False)
                nc.tensor.matmul(PS[:, c, :], w[1], x[0], start=False, stop=True).then_inc(st3.eup, 1)

        def edown_c(eng, i, e):
            wait(eng, st3.high, i, 2 * E, 2 * e + 2)
            wait(eng, st3.low, i, 2 * E, 2 * e + 2)
            wait(eng, st3.eacc, i, GROUP * E, GROUP * (e - 1))
            for j in range(GROUP):
                o = PS[:, 4 + e % 2, j * D:(j + 1) * D]
                nc.tensor.matmul(o, b2_ones, b2s[:, e, :], start=True, stop=False)
                for c in range(CH):
                    h = [hids[:, e % 2, k, c, j * T:(j + 1) * T] for k in range(2)]
                    w = [E2s[:, k, e, c, :] for k in range(2)]
                    nc.tensor.matmul(o, h[0], w[0], start=False, stop=False)
                    nc.tensor.matmul(o, h[0], w[1], start=False, stop=False)
                    last = nc.tensor.matmul(o, h[1], w[0], start=False, stop=c == CH - 1)
            last.then_inc(st3.edown, 1)

        def hidden_act(eng, i, e):
            wait(eng, st3.low, i, 2 * E, 2 * (e - 1))
            wait(eng, st3.edown, i, E, e - 1)
            for half in range(2):
                for c in (2 * half, 2 * half + 1):
                    wait(eng, st3.eup, i, CH * E, CH * e + c + 1)
                    nc.scalar.activation(hid32[:, e % 2, c, :], PS[:, c, :], ACT.Relu, bias=E1b[:, e, c:c + 1],
                                         scale=H_UP / (W_UP * X_UP)).then_inc(st3.relu, 1)
                wait(eng, st3.relu, i, CH * E, CH * e + 2 * half + 2)
                s = slice(2 * half, 2 * half + 2)
                nc.scalar.activation(hids[:, e % 2, 0, s, :], hid32[:, e % 2, s, :], ACT.Copy).then_inc(st3.high, 1)

        def low_dve(eng, i, e):
            wait(eng, st3.edown, i, E, e - 1)
            for half in range(2):
                wait(eng, st3.high, i, 2 * E, 2 * e + half + 1)
                s = slice(2 * half, 2 * half + 2)
                nc.vector.tensor_tensor(hids[:, e % 2, 1, s, :], hid32[:, e % 2, s, :], hids[:, e % 2, 0, s, :],
                                        ALU.subtract).then_inc(st3.low, 1)

        def acc_dve(eng, i, e):
            wait(eng, st3.edown, i, E, e + 1)
            wait(eng, st3.eacc, i, GROUP * E, GROUP * e)
            for j in range(GROUP):
                x = X[:, bass.ds(i * GROUP + j, 1), :]
                nc.vector.scalar_tensor_tensor(out=x, in0=PS[:, 4 + e % 2, j * D:(j + 1) * D].unsqueeze(1),
                                               scalar=gate[:, bass.ds(i * GROUP + j, 1), e], in1=x,
                                               op0=ALU.mult, op1=ALU.add).then_inc(st3.eacc, 1)

        def following(i, e, has_next):
            if e + 1 < E:
                return i, e + 1
            return (i + 1, 0) if has_next else None

        def pe_c(eng, i, has_prev, has_next):
            for e in range(E):
                after = following(i, e, has_next)
                if after:
                    eup_c(eng, *after)
                edown_c(eng, i, e)

        def dve_c(eng, i, has_prev, has_next):
            for e in range(E):
                after = following(i, e, has_next)
                if after:
                    low_dve(eng, *after)
                acc_dve(eng, i, e)

        def act_c(eng, i, has_prev, has_next):
            for e in range(E):
                hidden_act(eng, i, e)
                if isinstance(i, int) and i == 0 and e == 0:
                    gating_act(eng)

        def steps_c(eng, body):
            body(eng, 0, False, True)
            with eng.Fori(1, N - 1) as i:
                body(eng, i, True, True)
            body(eng, N - 1, True, False)

        def split_act(eng, k):
            if k == 0:
                eng.wait_ge(st.loads_moe, 16 * 4)
                nc.scalar.activation(E1s[:, 0, :, :], E1, ACT.Copy, scale=W_UP).then_inc(st3.split_high, 1)
            else:
                eng.wait_ge(st3.split_low, 1)
                nc.scalar.activation(E2s_flat[:, 0, :, :], E2, ACT.Copy, scale=W_UP).then_inc(st3.split_high, 1)

        def split_dve(eng, k):
            src, dst = ((E1, E1s), (E2, E2s_flat))[k]
            if k == 0:
                eng.wait_ge(st.loads_moe, 16 * 4)
                nc.vector.tensor_scalar(E1b[:, :, :], E1b[:, :, :], H_UP, None, ALU.mult).then_inc(st3.bias_prep, 1)
                nc.vector.memset(b2_ones, H_UP).then_inc(st3.bias_prep, 1)
                nc.vector.memset(b2s, 0.0).then_inc(st3.bias_prep, 1)
                nc.vector.tensor_scalar(b2_high, E2b[32:33, :, :], W_UP, None, ALU.mult).then_inc(st3.bias_prep, 1)
                eng.wait_ge(st3.bias_prep, 4)
                nc.vector.tensor_scalar(b2s[0:1, :, :], E2b[0:1, :, :], W_UP, None, ALU.mult).then_inc(st3.bias_prep, 1)
                nc.vector.scalar_tensor_tensor(out=b2s[32:33, :, :], in0=E2b[32:33, :, :], scalar=W_UP, in1=b2_high,
                                               op0=ALU.mult, op1=ALU.subtract).then_inc(st3.bias_prep, 1)
            eng.wait_ge(st3.split_high, k + 1)
            nc.vector.scalar_tensor_tensor(out=dst[:, 1, :, :], in0=src, scalar=W_UP, in1=dst[:, 0, :, :],
                                           op0=ALU.mult, op1=ALU.subtract).then_inc(st3.split_low, 1)

        kpad_ap = kpad.ap()
        KG_DVE = 8
        KG_CHAIN = 53
        block = ctx.enter_context(nc.Block())

        @block.sync
        def _(sp):
            def load(i):
                wait(sp, st.x_loaded, i, 16, 0)
                sp.dma_start(X[:, sl(i), :], t["x"][:, sl(i), :]).then_inc(st.x_loaded, 16)
                wait(sp, st.qkv, i, 3, 0)
                sp.dma_start(ctx_T[:, :], t["ctx"][:, bass.ds(i * GG, GG)]).then_inc(st.ctx_loaded, 16)
            load(0)
            for src, dst in ((t["Wq"], Wq[:, :]), (t["Wk"], Wk[:, :]), (t["Wv"], Wv[:, :])):
                sp.dma_start(dst, src).then_inc(st.loads_first, 16)
            sp.wait_ge(st.masks_clear, 1)
            for h in range(H):
                sp.dma_start(ctx_mask[h * DH:h * DH + 1, :], t["ctx_mask"]).then_inc(st.loads_first, 16)
            sp.dma_start(text_mask[:, :], t["text_mask"]).then_inc(st.loads_first, 16)
            sp.dma_start(WF[:, :], t["WF"]).then_inc(st.loads_first, 16)
            for r in (0, 32):
                sp.dma_start(film_bias[r:r + 1, :], t["bF"]).then_inc(st.loads_first, 16)
            for i in (1, 2):
                load(i)
            sp.wait_ge(st.consts, 9)
            sp.dma_start(kpad_ap[:, 0:T - 1], zero[:, 0:T - 1]).then_inc(st.kpad_written, 16)
            sp.wait_ge(st.kg_dve, KG_DVE)
            for q in range(4):
                sp.dma_start(bass.AP(tensor=kpad, offset=T - 1 + 32 * q * 2 * T, ap=[[HI, LO], [2 * T, 32], [1, HI]]),
                             kern[32 * q:32 * q + LO, :].rearrange("a (d b) -> a d b", b=HI)
                             ).then_inc(st.kpad_written, 16)
            sp.wait_ge(st.kpad_written, 16 * 5)
            for q in range(8):
                c = D // 8
                sp.dma_start(toep[:, q * c:(q + 1) * c, :],
                             bass.AP(tensor=kpad, offset=q * c * 2 * T, ap=[[1, T], [2 * T, c], [1, T]])
                             ).then_inc(st.toep_loaded, 16)
            with sp.Fori(3, N) as i:
                load(i)
            sp.wait_ge(st.conv, 8)
            sp.dma_start(E1, t["E1"]).then_inc(st.loads_moe, 16)
            sp.dma_start(E2, t["E2"]).then_inc(st.loads_moe, 16)
            for r in (0, 32):
                sp.dma_start(E2b[r:r + 1, :, :].rearrange("p e d -> p (e d)"), t["E2b"]).then_inc(st.loads_moe, 16)
            with sp.Fori(0, N) as i:
                wait(sp, st3.eacc, i, GROUP * E, GROUP * E)
                sp.dma_start(out[:, sl(i), :], X[:, sl(i), :]).then_inc(st3.stored, 16)
            sp.wait_ge(st3.stored, 16 * N)

        @block.gpsimd
        def _(pool):
            nc.gpsimd.memset(ident[:, :], 0.0).then_inc(st.consts, 1)
            nc.gpsimd.memset(ones[:, :], 1.0).then_inc(st.consts, 1)
            nc.gpsimd.memset(mhalf[:, :], -0.5).then_inc(st.consts, 1)
            nc.gpsimd.memset(zero[:, :], 0.0).then_inc(st.consts, 1)
            nc.gpsimd.memset(eps[:, :], EPS).then_inc(st.consts, 1)
            nc.gpsimd.memset(anti[:, :], 0.0).then_inc(st.consts, 1)
            nc.gpsimd.iota(steps_i[:, 0:LO], [[HI, LO]], base=0, channel_multiplier=0).then_inc(st.consts, 1)
            nc.gpsimd.iota(steps_i[:, LO:NL], [[1, HI]], base=0, channel_multiplier=0).then_inc(st.consts, 1)
            nc.gpsimd.iota(eid_i[:, :], [[1, E]], base=0, channel_multiplier=0).then_inc(st.consts, 1)
            pool.wait_ge(st.consts, 9)
            nc.gpsimd.affine_select(out=ident[:, :], in_=ident[:, :], compare_op=ALU.not_equal, fill=1.0, base=0,
                                    pattern=[[-1, 128]], channel_multiplier=1).then_inc(st.consts, 1)
            nc.gpsimd.affine_select(out=anti[:, :], in_=anti[:, :], compare_op=ALU.not_equal, fill=1.0, base=-127,
                                    pattern=[[1, 128]], channel_multiplier=1).then_inc(st.consts, 1)
            nc.gpsimd.tensor_copy(steps[:, :], steps_i[:, :]).then_inc(st.consts, 1)
            nc.gpsimd.tensor_copy(eid[:, :], eid_i[:, :]).then_inc(st.consts, 1)
            pool.wait_ge(st.consts, 13)
            pool.wait_ge(st.masks, 8)
            rstd_a(pool, 0)
            pool.wait_ge(st.loads_first, 16 * 12)
            affine_a(pool, 0)
            steps_of(pool, pool_a)
            norm_factors(pool, 0, mv1, rs1, st2.s1, st2.r1, st2.n1)
            pool.wait_ge(st2.prep_pool, 4)
            steps_of(pool, pool_b)
            norm_factors(pool, N - 1, mv3, rs3, st2.s3, st2.r3, st2.n3)

        @block.scalar
        def _(act):
            act.dma_start(TOEP[:, 0:4 * D], t["AC"]).then_inc(st.loads_kernel, 16)
            act.dma_start(kg["ldt"], t["ldt"].to_broadcast([128, D])).then_inc(st.loads_kernel, 16)
            act.dma_start(row_params[:, :], t["row_params"].to_broadcast([128, 4 * D + 3])).then_inc(st.loads_first, 16)
            act.wait_ge(st.masks_clear, 2)
            for q in range(4):
                act.dma_start(dskip[32 * q:32 * q + 1, :], t["dskip"][:, 32 * q:32 * q + 32]).then_inc(st.loads_skip, 16)
            act.wait_ge(st.loads_kernel, 16 * 2)
            nc.scalar.activation(kg["dt"], kg["ldt"], ACT.Exp).then_inc(st.kg_act, 1)
            act.dma_start(W1[:, :], t["W1"]).then_inc(st.loads_mlp, 16)
            act.dma_start(W2[:, :, :], t["W2"]).then_inc(st.loads_mlp, 16)
            act.dma_start(b1[:, :], t["b1"]).then_inc(st.loads_mlp, 16)
            act.dma_start(b2row[:, :], t["b2"]).then_inc(st.loads_mlp, 16)
            act.dma_start(g_ffn[:, :], t["g_ffn"]).then_inc(st.loads_mlp, 16)
            act.dma_start(b_ffn[:, :], t["b_ffn"]).then_inc(st.loads_mlp, 16)
            act.dma_start(RW[:, :], t["RW"]).then_inc(st.loads_mlp, 16)
            act.dma_start(E1b[:, :, :], t["E1b"]).then_inc(st.loads_mlp, 16)
            act.wait_ge(st.kg_chain, 1)
            nc.scalar.activation(kg["th"], kg["re"], ACT.Tanh, scale=0.5).then_inc(st.kg_act, 1)
            for k, l in enumerate([HI * a for a in range(LO)] + list(range(HI))):
                nc.scalar.activation(kg["mag"][:, :, k], kg["re"], ACT.Exp, scale=float(l)).then_inc(st.kg_mag, 1)
            act.wait_ge(st.kg_chain, 16)
            for name in ("s2", "c2", "sa", "sb"):
                nc.scalar.activation(kg[name], kg[name], ACT.Sin, scale=TWO_PI).then_inc(st.kg_act, 1)
            norm_a(act, 0)
            trev_a(act, 0)
            qkvev_a(act, 0)
            vev_a(act, 0)
            for h in range(3):
                s_a(act, 0, h)
            steps_of(act, act_a)
            attnTev_a(act, N - 1)
            cTev_a(act, N - 1)
            fo_a(act, N - 1, range(GROUP))
            act.wait_ge(st.loads_mlp, 16 * 8)
            nc.scalar.activation(W1g[:, :], W1[:, :], ACT.Copy, scale=g_ffn[:, :]).then_inc(st2.prep_act, 1)
            nc.scalar.activation(gates[:, :], gates[:, :], ACT.Tanh).then_inc(st2.prep_act, 1)
            for g in range(0, N, 2):
                act.wait_ge(st.rev, g + 1)
                nc.scalar.activation(XIN[:, g * GROUP:(g + 1) * GROUP, :], PS[:, g, :].rearrange(
                    "p (j d) -> p j d", j=GROUP), ACT.Copy).then_inc(st.rev_act, 1)
            for q in range(0, 8, 2):
                act.wait_ge(st.conv, q + 1)
                nc.scalar.activation(Y[:, :, 16 * q:16 * q + 16], PS[:, q, :].rearrange("p (d b) -> p b d", b=B),
                                     ACT.Copy).then_inc(st.y_ready, 1)
            n1_b(act, 0)
            tr1ev_b(act, 0)
            steps_of(act, act_b, (lambda: split_act(act, 0), lambda: split_act(act, 1)))
            n2_b(act, N - 1)
            n3_b(act, N - 1)
            tr3ev_b(act, N - 1)
            act.wait_ge(st3.split_low, 2)
            act.wait_ge(st2.xt, 3 * N)
            act.wait_ge(st3.bias_prep, 1)
            steps_c(act, act_c)

        @block.vector
        def _(dve):
            nc.vector.memset(ctx_mask[:, :], 0).then_inc(st.masks_clear, 1)
            nc.vector.memset(dskip[:, :], 0.0).then_inc(st.masks_clear, 1)
            nc.vector.memset(ones_bf[:, :], 1.0).then_inc(st.masks, 1)
            nc.vector.memset(minus1[:, :], -1.0).then_inc(st.masks, 1)
            for p, first, second, two in ((0, 0.25, 0.0, 2.0), (64, 0.0, 0.25, -2.0)):
                nc.vector.memset(quarter[p:p + 64, 0:1], first).then_inc(st.masks, 1)
                nc.vector.memset(quarter[p:p + 64, 1:2], second).then_inc(st.masks, 1)
                nc.vector.memset(sign2[p:p + 64, :], two).then_inc(st.masks, 1)
            n = 0

            def link(ins):
                nonlocal n
                n += 1
                ins.then_inc(st.kg_chain, 1)
                dve.wait_ge(st.kg_chain, n)

            def tt(o, a, b, op):
                link(nc.vector.tensor_tensor(kg[o], kg[a], kg[b], op))

            def ts(o, a, s1, op1, s2=None, op2=ALU.bypass):
                link(nc.vector.tensor_scalar(kg[o], kg[a], s1, s2, op1, op2))

            dve.wait_ge(st.consts, 13)
            dve.wait_ge(st.loads_kernel, 16 * 2)
            dve.wait_ge(st.kg_act, 1)
            tt("re", "are", "dt", ALU.mult)
            tt("t0", "aim", "dt", ALU.mult)
            ts("tu", "t0", INV_TWO_PI, ALU.mult)
            ts("t0", "tu", 0.5, ALU.mult)
            ts("t1", "t0", ROUND, ALU.add, -ROUND, ALU.add)
            tt("s2", "t0", "t1", ALU.subtract)
            ts("t0", "t0", 0.25, ALU.add)
            ts("t1", "t0", ROUND, ALU.add, -ROUND, ALU.add)
            tt("c2", "t0", "t1", ALU.subtract)
            assert n == 9
            stp = steps[:, :].unsqueeze(1).to_broadcast([128, D, NL])
            link(nc.vector.tensor_tensor(kg["sa"], kg["tu"].unsqueeze(2).to_broadcast([128, D, NL]), stp, ALU.mult))
            link(nc.vector.tensor_scalar(kg["tb"], kg["sa"][:, :, 0:LO], quarter[:, 1:2], None, ALU.add))
            link(nc.vector.tensor_scalar(kg["sa"], kg["sa"], quarter[:, 0:1], None, ALU.add))
            link(nc.vector.tensor_scalar(kg["ta"], kg["sa"], ROUND, -ROUND, ALU.add, ALU.add))
            link(nc.vector.tensor_tensor(kg["sa"], kg["sa"], kg["ta"], ALU.subtract))
            link(nc.vector.tensor_scalar(kg["sb"], kg["tb"], ROUND, -ROUND, ALU.add, ALU.add))
            link(nc.vector.tensor_tensor(kg["sb"], kg["tb"], kg["sb"], ALU.subtract))
            assert n == 16
            stats_a(dve, 0)
            dve.wait_ge(st.loads_first, 16 * 12)
            nc.vector.tensor_scalar(text_w[:, :], text_mask[:, :], 1.0 / H, None, ALU.mult).then_inc(st.masks, 1)
            bias_a(dve, 0)
            nc.vector.tensor_scalar(WF[:, :], WF[:, :], mod[:, :], None, ALU.mult).then_inc(st.film_params, 1)
            nc.vector.memset(film_row[:, 0, :], 0.0).then_inc(st.film_params, 1)
            nc.vector.memset(part_ones[:, :], 1.0).then_inc(st.film_params, 1)
            for r in (0, 32):
                b = film_bias[r:r + 1, :]
                nc.vector.tensor_scalar(b, b, mod[r:r + 1, :], None, ALU.mult).then_inc(st.film_params, 1)
            dve.wait_ge(st.film_params, 5)
            for r in (0, 32):
                for k in range(2):
                    b = film_bias[r:r + 1, 2 * k * D:(2 * k + 1) * D]
                    nc.vector.tensor_scalar(b, b, 1.0, None, ALU.add).then_inc(st.film_params, 1)
            dve.wait_ge(st.film_params, 9)
            for r in (0, 32):
                nc.vector.tensor_copy(film_row[r:r + 1, r // 32, :], film_bias[r:r + 1, :]).then_inc(st.film_params, 1)
            dve.wait_ge(st.film_params, 11)
            nc.vector.tensor_tensor(film_row[32:33, 0, :], film_bias[32:33, :], film_row[32:33, 1, :],
                                    ALU.subtract).then_inc(st.film_params, 1)
            tt("t0", "are", "are", ALU.mult)
            tt("t1", "aim", "aim", ALU.mult)
            tt("t0", "t0", "t1", ALU.add)
            link(nc.vector.reciprocal(kg["t2"], kg["t0"]))
            dve.wait_ge(st.kg_act, 2)
            ts("t0", "th", -1.0, ALU.mult, 1.0, ALU.add)
            link(nc.vector.reciprocal(kg["t0"], kg["t0"]))
            tt("em", "th", "t0", ALU.mult)
            ts("em", "em", 2.0, ALU.mult)
            dve.wait_ge(st.kg_act, 6)
            tt("q", "s2", "s2", ALU.mult)
            ts("q", "q", 2.0, ALU.mult)
            ts("t0", "q", -1.0, ALU.mult, 1.0, ALU.add)
            tt("t0", "em", "t0", ALU.mult)
            tt("nr", "t0", "q", ALU.subtract)
            tt("t1", "s2", "c2", ALU.mult)
            ts("t0", "em", 1.0, ALU.add, 2.0, ALU.mult)
            tt("ni", "t0", "t1", ALU.mult)
            tt("t0", "cre", "nr", ALU.mult)
            tt("t1", "cim", "ni", ALU.mult)
            tt("xr", "t0", "t1", ALU.subtract)
            tt("t0", "cre", "ni", ALU.mult)
            tt("t1", "cim", "nr", ALU.mult)
            tt("xi", "t0", "t1", ALU.add)
            tt("t0", "xr", "are", ALU.mult)
            tt("t1", "xi", "aim", ALU.mult)
            tt("t0", "t0", "t1", ALU.add)
            tt("t0", "t0", "t2", ALU.mult)
            link(nc.vector.tensor_scalar(kg["P"], kg["t0"], sign2[:, :], None, ALU.mult))
            tt("t0", "xi", "are", ALU.mult)
            tt("t1", "xr", "aim", ALU.mult)
            tt("t0", "t0", "t1", ALU.subtract)
            tt("t0", "t0", "t2", ALU.mult)
            ts("Q", "t0", -2.0, ALU.mult)
            dve.wait_ge(st.kg_mag, NL)
            link(nc.vector.tensor_tensor(kg["sa"], kg["sa"], kg["mag"], ALU.mult))
            link(nc.vector.tensor_tensor(kg["sb"], kg["sb"], kg["mag"][:, :, 0:LO], ALU.mult))
            link(nc.vector.tensor_tensor(kg["U"], kg["sa"][:, :, 0:LO], kg["P"].unsqueeze(2).to_broadcast([128, D, LO]),
                                         ALU.mult))
            link(nc.vector.tensor_tensor(kg["u2"], kg["sb"], kg["Q"].unsqueeze(2).to_broadcast([128, D, LO]), ALU.mult))
            link(nc.vector.tensor_tensor(kg["U"], kg["U"], kg["u2"], ALU.add))
            assert n == KG_CHAIN, n
            def kernel_out():
                dve.wait_ge(st.kg_mm, 1)
                dve.wait_ge(st.loads_skip, 16 * 4)
                for q in range(4):
                    o = slice(32 * q, 32 * q + LO)
                    nc.vector.tensor_copy(kern[o, :], PS[o, 3, :]).then_inc(st.kg_dve, 1)
                dve.wait_ge(st.kg_dve, 4)
                k0 = kern[:, :].rearrange("a (d b) -> a d b", b=HI)[:, :, 0]
                for q in range(4):
                    o = slice(32 * q, 32 * q + LO)
                    nc.vector.tensor_tensor(k0[o, :], k0[o, :], dskip[o, :], ALU.add).then_inc(st.kg_dve, 1)
            steps_of(dve, dve_a, (kernel_out,))
            xin_a(dve, N - 1, range(GROUP))
            dve.wait_ge(st2.prep_act, 2)
            nc.vector.tensor_scalar(g_out[:, :], g_out[:, :], gates[:, 0:1], None, ALU.mult).then_inc(st2.prep_pool, 1)
            nc.vector.tensor_scalar(b_out[:, :], b_out[:, :], gates[:, 0:1], None, ALU.mult).then_inc(st2.prep_pool, 1)
            for g in range(1, N, 2):
                dve.wait_ge(st.rev, g + 1)
                nc.vector.tensor_copy(XIN[:, g * GROUP:(g + 1) * GROUP, :], PS[:, g, :].rearrange(
                    "p (j d) -> p j d", j=GROUP)).then_inc(st.rev_dve, 1)
            for q in range(1, 8, 2):
                dve.wait_ge(st.conv, q + 1)
                nc.vector.tensor_copy(Y[:, :, 16 * q:16 * q + 16], PS[:, q, :].rearrange("p (d b) -> p b d", b=B)
                                      ).then_inc(st.y_ready, 1)
            dve.wait_ge(st2.prep_pe, 1)
            nc.vector.tensor_tensor(b1p[:, :], b1[:, :], PS[:, 7, 0:CH], ALU.add).then_inc(st2.prep_pool, 1)
            nc.vector.memset(zero[:, 0:1], 0.0).then_inc(st2.prep_pool, 1)
            xt_b(dve, 0)
            steps_of(dve, dve_b, (lambda: split_dve(dve, 0), lambda: split_dve(dve, 1)))
            x1_b(dve, N - 1)
            logit_b(dve, N - 1)
            keep_b(dve, N - 1)
            dve.wait_ge(st2.logit, N)
            low_dve(dve, 0, 0)
            gating_dve(dve)
            steps_c(dve, dve_c)

        @block.tensor
        def _(pe):
            pe.wait_ge(st.consts, 11)
            tr_a(pe, 0)
            pe.wait_ge(st.loads_first, 16 * 12)
            pe.wait_ge(st.masks, 1)
            qkv_a(pe, 0)
            for h in range(H):
                scores_a(pe, 0, h)
            pe.wait_ge(st.kg_chain, KG_CHAIN)
            for d in range(D):
                q, r = d // 32, d % 32
                last = nc.tensor.matmul(PS[32 * q:32 * q + LO, 3, r * HI:(r + 1) * HI], kg["U"][:, d, :],
                                        kg["sa"][:, d, LO:NL], start=True, stop=True, skip_group_check=True)
            last.then_inc(st.kg_mm, 1)
            pe.wait_ge(st.film_params, 12)
            steps_of(pe, pe_a, (lambda: pe.wait_ge(st.kg_dve, 4),))
            attnT_a(pe, N - 1)
            cT_a(pe, N - 1)
            film_a(pe, N - 1)
            pe.wait_ge(st.toep_loaded, 16 * 8)
            pe.wait_ge(st.xin, N * PER["xin"])
            pe.wait_ge(st.fo, N * GROUP)
            pe.wait_ge(st.S_ready, N * H)
            for g in range(N):
                nc.tensor.matmul(PS[:, g, :], anti[:, :], XIN[:, g * GROUP:(g + 1) * GROUP, :], start=True,
                                 stop=True).then_inc(st.rev, 1)
            pe.wait_ge(st.rev_act, N // 2)
            pe.wait_ge(st.rev_dve, N // 2)
            for d in range(D):
                q, r = d // 16, d % 16
                last = nc.tensor.matmul(PS[:, q, r * B:(r + 1) * B], toep[:, d, :], XIN[:, :, d], start=True, stop=True)
                if r == 15:
                    last.then_inc(st.conv, 1)
            pe.wait_ge(st.y_ready, 8)
            pe.wait_ge(st.loads_mlp, 16 * 8)
            for c in range(CH):
                last = nc.tensor.matmul(PS[:, 7, c:c + 1], W1[:, c * 128:(c + 1) * 128], b_ffn[:, :], start=True, stop=True)
            last.then_inc(st2.prep_pe, 1)
            tr1_b(pe, 0)
            pe.wait_ge(st2.prep_pool, 4)
            pe.wait_ge(st2.prep_act, 1)
            steps_of(pe, pe_b)
            tr3_b(pe, N - 1)
            route_b(pe, N - 1)
            pe.wait_ge(st2.x3keep, N)
            pe.wait_ge(st2.xt2, N)
            pe.wait_ge(st3.split_low, 2)
            pe.wait_ge(st3.bias_prep, 6)
            eup_c(pe, 0, 0)
            steps_c(pe, pe_c)


def kernel(**inputs):
    import numpy as np
    import concourse.bacc as bacc
    from concourse.bass_utils import run_bass_kernel_spmd

    a = {k: np.asarray(v) for k, v in inputs.items()}
    p = "L0_xattn_"
    row = lambda v: v.reshape(1, -1)
    data = {
        "x": a["x"].transpose(1, 0, 2),
        "ctx": a["ctx_768"].transpose(2, 0, 1).reshape(DV, B * G),
        "text_mask": a["mask_BxS_bf1"].view(np.uint8).T,
        "ctx_mask": a["mask_BxS2_bf1"].view(np.uint8).reshape(1, B * G),
        "Wq": a[p + "Wq"], "Wk": a[p + "Wk"], "Wv": a[p + "Wv"],
        "WF": np.concatenate([a[p + "W_film_in"], a[p + "W_film_out"]], axis=1),
        "bF": row(np.concatenate([a[p + "b_film_in"], a[p + "b_film_out"]])),
        "row_params": row(np.concatenate([a[p + "g_norm_in"], a[p + "b_norm_in"], a[p + "g_norm_out"],
                                          a[p + "b_norm_out"], a[p + "mod_gate"].reshape(1),
                                          a["g_xattn"].reshape(1), a["g_ffn"].reshape(1)])),
        "g_ffn": a[p + "g_ffn"].reshape(D, 1), "b_ffn": a[p + "b_ffn"].reshape(D, 1),
        "W1": a[p + "W1"], "b1": a[p + "b1"].reshape(CH, 128).T,
        "W2": a[p + "W2"].reshape(CH, 128, D).transpose(1, 0, 2), "b2": row(a[p + "b2"]),
        "ldt": row(a[p + "log_dt"]),
        "AC": np.concatenate(2 * [np.concatenate([a[p + n].T for n in ("A_re", "A_im", "C_re", "C_im")], axis=1)]),
        "dskip": row(a[p + "D_skip"]),
        "RW": a["L0_ffn_router_w"].T,
        "E1": a["L0_ffn_w1"].transpose(2, 0, 1),
        "E1b": a["L0_ffn_b1"].reshape(E, CH, 128).transpose(2, 0, 1),
        "E2": a["L0_ffn_w2"].reshape(E, D, CH, 128).transpose(3, 0, 2, 1).reshape(128, E, HID),
        "E2b": row(a["L0_ffn_b2"]),
    }
    nc = bacc.Bacc("TRN2", target_bir_lowering=False, num_devices=1)
    arrays, t = {}, {}
    for name, v in data.items():
        v = np.ascontiguousarray(v)
        arrays[f"in_{name}"] = v
        t[name] = nc.dram_tensor(f"in_{name}", v.shape, mybir.dt.from_np(v.dtype), kind="ExternalInput").ap()
    out = nc.dram_tensor("out", (T, B, D), F32, kind="ExternalOutput").ap()
    build(nc, t, out)
    r = run_bass_kernel_spmd(nc, [arrays], core_ids=[0])
    return np.ascontiguousarray(r.results[0]["out"].transpose(1, 0, 2))
```
